# Optimizing a Trainium2 kernel written in Bass

```python
import numpy as np
import jax
import jax.numpy as jnp

def _softmax(x, axis=-1):
    return jax.nn.softmax(x, axis=axis)

def _gelu(x):
    return jax.nn.gelu(x, approximate=True)

def _silu(x):
    return jax.nn.silu(x)

def _sigmoid(x):
    return jax.nn.sigmoid(x)

def _layernorm(x, axis=-1, eps=1e-05):
    m = jnp.mean(x, axis=axis, keepdims=True)
    v = jnp.var(x, axis=axis, keepdims=True)
    return (x - m) / jnp.sqrt(v + eps)

def _scatter_add(tgt, idx, src, axis=0):
    return tgt.at[idx].add(src)

def _segment_sum(src, seg, n):
    return jax.ops.segment_sum(src, seg, n)
kernel_name = 'mk_seq_postln_d2_jaxref_r8_ea6442'

def setup_inputs(seed: int=0):
    np.random.seed(seed)
    _w = jnp.asarray

    def _L0_attn_setup():
        import jax, jax.numpy as jnp
        import numpy as np
        N_EMBD = 128
        N_HEAD = 8
        HEAD_DIM = N_EMBD // N_HEAD
        EPS = 1e-06

        def _lrpe(xh, theta, n):
            idx = jnp.arange(n, dtype=xh.dtype).reshape(1, n, 1)
            th = theta * idx
            th = th[None]
            return jnp.concatenate([xh * jnp.cos(th), xh * jnp.sin(th)], axis=-1)

        def _srmsnorm(y):
            ms = jnp.mean(jnp.square(y), axis=-1, keepdims=True)
            return y * jax.lax.rsqrt(ms + EPS)
        key = jax.random.key(seed)
        ks = jax.random.split(key, 8)
        b, n = (2, 256)
        x = jax.random.normal(ks[0], (b, n, N_EMBD), dtype=jnp.float32)
        slope_rate = -jax.random.uniform(ks[1], (N_HEAD, 1, 1), dtype=jnp.float32)
        s = 0.02
        qkvu_w = jax.random.normal(ks[2], (4 * N_EMBD, N_EMBD), dtype=jnp.float32) * s
        qkvu_b = jnp.zeros((4 * N_EMBD,), dtype=jnp.float32)
        out_w = jax.random.normal(ks[3], (N_EMBD, N_EMBD), dtype=jnp.float32) * s
        out_b = jnp.zeros((N_EMBD,), dtype=jnp.float32)
        d = N_EMBD
        theta = (10000.0 ** (-2.0 / d * jnp.arange(d, dtype=jnp.float32))).reshape(N_HEAD, 1, HEAD_DIM)
        return {'x': x, 'slope_rate': slope_rate, 'qkvu_w': qkvu_w, 'qkvu_b': qkvu_b, 'out_w': out_w, 'out_b': out_b, 'theta': theta}
    _L0_attn_in = _L0_attn_setup()

    def _L0_ffn_setup():
        import jax, jax.numpy as jnp
        import numpy as np
        DIM = 128
        DEPTH = 2
        HEADS = 8
        DIM_HEAD = 64
        WINDOW = 64
        INNER = HEADS * DIM_HEAD
        HID = int(DIM * 4 * 2 / 3)
        B, N = (2, 1024)
        QK_SCALE = 8.0

        def shift_token(t):
            t1, t2 = jnp.split(t, 2, axis=-1)
            t2 = jnp.pad(t2, ((0, 0), (1, 0), (0, 0)))[:, :-1]
            return jnp.concatenate([t1, t2], axis=-1)

        def l2norm(t):
            return t / jnp.clip(jnp.linalg.norm(t, axis=-1, keepdims=True), 1e-12)

        def rotate_half(x):
            x1, x2 = jnp.split(x, 2, axis=-1)
            return jnp.concatenate([-x2, x1], axis=-1)

        def rotary_xpos(q, k):
            n = q.shape[-2]
            half_idx = jnp.arange(0, DIM_HEAD, 2, dtype=jnp.float32)
            inv_freq = 1.0 / 10000.0 ** (half_idx / DIM_HEAD)
            t = jnp.arange(n, dtype=jnp.float32)
            freqs = t[:, None] * inv_freq[None, :]
            freqs = jnp.concatenate([freqs, freqs], axis=-1)
            base = (half_idx + 0.4 * DIM_HEAD) / (1.4 * DIM_HEAD)
            power = (t - n // 2) / float(WINDOW // 2)
            scale = base[None, :] ** power[:, None]
            scale = jnp.concatenate([scale, scale], axis=-1)
            cos, sin = (jnp.cos(freqs), jnp.sin(freqs))
            q = q * cos * scale + rotate_half(q) * sin * scale
            k = k * cos / scale + rotate_half(k) * sin / scale
            return (q, k)

        def local_attention(q, k, v):
            b, h, n, d = q.shape
            w = n // WINDOW
            bq = q.reshape(b, h, w, WINDOW, d) * QK_SCALE
            bk = k.reshape(b, h, w, WINDOW, d)
            bv = v.reshape(b, h, w, WINDOW, d)

            def look_around(t):
                p = jnp.pad(t, ((0, 0), (0, 0), (1, 0), (0, 0), (0, 0)))
                return jnp.concatenate([p[:, :, :w], p[:, :, 1:]], axis=3)
            bk, bv = (look_around(bk), look_around(bv))
            bt = jnp.arange(n).reshape(w, WINDOW)
            btp = jnp.pad(bt, ((1, 0), (0, 0)), constant_values=-1)
            btk = jnp.concatenate([btp[:w], btp[1:]], axis=1)
            sim = jnp.einsum('bhwid,bhwjd->bhwij', bq, bk)
            i = bt[:, :, None]
            j = btk[:, None, :]
            mask = (i < j) | (i > j + WINDOW) | (j == -1)
            sim = jnp.where(mask, -jnp.finfo(sim.dtype).max, sim)
            attn = jax.nn.softmax(sim, axis=-1)
            out = jnp.einsum('bhwij,bhwjd->bhwid', attn, bv)
            return out.reshape(b, h, n, d)

        def _layer(x, wqkv, qs, ksc, wo, lg, lb, w1, b1, w2, b2):
            b, n, _ = x.shape
            h = shift_token(x)
            qkv = h @ wqkv
            q, k, v = jnp.split(qkv, 3, axis=-1)
            to_heads = lambda t: t.reshape(b, n, HEADS, DIM_HEAD).transpose(0, 2, 1, 3)
            q, k, v = (to_heads(q), to_heads(k), to_heads(v))
            q = l2norm(q) * qs
            k = l2norm(k) * ksc
            q, k = rotary_xpos(q, k)
            o = local_attention(q, k, v)
            o = o.transpose(0, 2, 1, 3).reshape(b, n, INNER)
            x = x + o @ wo
            h = shift_token(x)
            mu = h.mean(-1, keepdims=True)
            var = h.var(-1, keepdims=True)
            h = (h - mu) / jnp.sqrt(var + 1e-05) * lg + lb
            h = h @ w1 + b1
            a, g = jnp.split(h, 2, axis=-1)
            h = a * jax.nn.gelu(g, approximate=False)
            x = x + h @ w2 + b2
            return x
        key = jax.random.key(seed)
        ks = jax.random.split(key, 6)
        return {'x': jax.random.normal(ks[0], (B, N, DIM), jnp.float32), 'wqkv': jax.random.normal(ks[1], (DEPTH, DIM, 3 * INNER), jnp.float32) * 0.02, 'q_scale': jnp.ones((DEPTH, DIM_HEAD), jnp.float32), 'k_scale': jnp.ones((DEPTH, DIM_HEAD), jnp.float32), 'wo': jax.random.normal(ks[2], (DEPTH, INNER, DIM), jnp.float32) * 0.02, 'ln_g': jnp.ones((DEPTH, DIM), jnp.float32), 'ln_b': jnp.zeros((DEPTH, DIM), jnp.float32), 'w1': jax.random.normal(ks[3], (DEPTH, DIM, 2 * HID), jnp.float32) * 0.02, 'b1': jnp.zeros((DEPTH, 2 * HID), jnp.float32), 'w2': jax.random.normal(ks[4], (DEPTH, HID, DIM), jnp.float32) * 0.02, 'b2': jnp.zeros((DEPTH, DIM), jnp.float32)}
    _L0_ffn_in = _L0_ffn_setup()

    def _L1_attn_setup():
        import jax, jax.numpy as jnp
        import numpy as np
        B, L, C = (4, 128, 128)
        H = 8
        D = C // H
        MAX_SAMPLES = 32
        HALF_S = MAX_SAMPLES // 2
        S = 2 * HALF_S + 1
        K = 64
        MAX_FREQ = 16.0
        MIN_FREQ = 1.0

        def _silu(v):
            return v * jax.nn.sigmoid(v)
        key = jax.random.key(seed)
        ks = jax.random.split(key, 6)
        x = jax.random.normal(ks[0], (B, L, C), dtype=jnp.float32)
        wave_w = jax.random.normal(ks[1], (2 * H, C), dtype=jnp.float32) * 0.02
        wave_b = jnp.zeros((2 * H,), dtype=jnp.float32)
        kernel_w = jax.random.normal(ks[2], (H * K, C), dtype=jnp.float32) * (0.1 / np.sqrt(C))
        kernel_b = jnp.zeros((H * K,), dtype=jnp.float32)
        out_w = jax.random.normal(ks[3], (C, C), dtype=jnp.float32) * (0.1 / np.sqrt(C))
        return {'x': x, 'wave_w': wave_w, 'wave_b': wave_b, 'kernel_w': kernel_w, 'kernel_b': kernel_b, 'out_w': out_w}
    _L1_attn_in = _L1_attn_setup()

    def _L1_ffn_setup():
        import jax, jax.numpy as jnp
        import numpy as np
        K = 2
        key = jax.random.key(seed)
        ks = jax.random.split(key, 9)
        B, S, D, O, E = (4, 128, 128, 128, 8)
        sc = 0.02
        return {'x': jax.random.normal(ks[0], (B, S, D), dtype=jnp.float32), 'gate_w': jax.random.normal(ks[1], (D, E), dtype=jnp.float32) * sc, 'gate_b': jax.random.normal(ks[2], (E,), dtype=jnp.float32) * sc, 'w1': jax.random.normal(ks[3], (E, D, O), dtype=jnp.float32) * sc, 'b1': jax.random.normal(ks[4], (E, O), dtype=jnp.float32) * sc, 'w2': jax.random.normal(ks[5], (E, O, O), dtype=jnp.float32) * sc, 'b2': jax.random.normal(ks[6], (E, O), dtype=jnp.float32) * sc, 'w3': jax.random.normal(ks[7], (E, O, O), dtype=jnp.float32) * sc, 'b3': jax.random.normal(ks[8], (E, O), dtype=jnp.float32) * sc}
    _L1_ffn_in = _L1_ffn_setup()
    _d = {'L0_attn_x': _L0_attn_in['x'], 'L0_attn_slope_rate': _L0_attn_in['slope_rate'], 'L0_attn_qkvu_w': _L0_attn_in['qkvu_w'], 'L0_attn_qkvu_b': _L0_attn_in['qkvu_b'], 'L0_attn_out_w': _L0_attn_in['out_w'], 'L0_attn_out_b': _L0_attn_in['out_b'], 'L0_attn_theta': _L0_attn_in['theta'], 'L0_ffn_wqkv': _L0_ffn_in['wqkv'], 'L0_ffn_q_scale': _L0_ffn_in['q_scale'], 'L0_ffn_k_scale': _L0_ffn_in['k_scale'], 'L0_ffn_wo': _L0_ffn_in['wo'], 'L0_ffn_ln_g': _L0_ffn_in['ln_g'], 'L0_ffn_ln_b': _L0_ffn_in['ln_b'], 'L0_ffn_w1': _L0_ffn_in['w1'], 'L0_ffn_b1': _L0_ffn_in['b1'], 'L0_ffn_w2': _L0_ffn_in['w2'], 'L0_ffn_b2': _L0_ffn_in['b2'], 'L1_attn_wave_w': _L1_attn_in['wave_w'], 'L1_attn_wave_b': _L1_attn_in['wave_b'], 'L1_attn_kernel_w': _L1_attn_in['kernel_w'], 'L1_attn_kernel_b': _L1_attn_in['kernel_b'], 'L1_attn_out_w': _L1_attn_in['out_w'], 'L1_ffn_gate_w': _L1_ffn_in['gate_w'], 'L1_ffn_gate_b': _L1_ffn_in['gate_b'], 'L1_ffn_w1': _L1_ffn_in['w1'], 'L1_ffn_b1': _L1_ffn_in['b1'], 'L1_ffn_w2': _L1_ffn_in['w2'], 'L1_ffn_b2': _L1_ffn_in['b2'], 'L1_ffn_w3': _L1_ffn_in['w3'], 'L1_ffn_b3': _L1_ffn_in['b3']}
    _x0 = _d['L0_attn_x']
    _d['L0_attn_x'] = jax.random.normal(jax.random.fold_in(jax.random.key(seed), 1), (4, 1024, 128), dtype=_x0.dtype)
    del _x0
    return _d

def reference(L0_attn_x, L0_attn_slope_rate, L0_attn_qkvu_w, L0_attn_qkvu_b, L0_attn_out_w, L0_attn_out_b, L0_attn_theta, L0_ffn_wqkv, L0_ffn_q_scale, L0_ffn_k_scale, L0_ffn_wo, L0_ffn_ln_g, L0_ffn_ln_b, L0_ffn_w1, L0_ffn_b1, L0_ffn_w2, L0_ffn_b2, L1_attn_wave_w, L1_attn_wave_b, L1_attn_kernel_w, L1_attn_kernel_b, L1_attn_out_w, L1_ffn_gate_w, L1_ffn_gate_b, L1_ffn_w1, L1_ffn_b1, L1_ffn_w2, L1_ffn_b2, L1_ffn_w3, L1_ffn_b3):

    def _L0_attn_ref(x, slope_rate, qkvu_w, qkvu_b, out_w, out_b, theta):
        import jax, jax.numpy as jnp
        import numpy as np
        N_EMBD = 128
        N_HEAD = 8
        HEAD_DIM = N_EMBD // N_HEAD
        EPS = 1e-06

        def _lrpe(xh, theta, n):
            idx = jnp.arange(n, dtype=xh.dtype).reshape(1, n, 1)
            th = theta * idx
            th = th[None]
            return jnp.concatenate([xh * jnp.cos(th), xh * jnp.sin(th)], axis=-1)

        def _srmsnorm(y):
            ms = jnp.mean(jnp.square(y), axis=-1, keepdims=True)
            return y * jax.lax.rsqrt(ms + EPS)
        b, n, hd = x.shape
        h = N_HEAD
        qkvu = x @ qkvu_w.T + qkvu_b
        q, k, v, u = jnp.split(qkvu, 4, axis=-1)

        def to_heads(t):
            return t.reshape(b, n, h, hd // h).transpose(0, 2, 1, 3)
        q, k, v = (to_heads(q), to_heads(k), to_heads(v))
        q = jax.nn.silu(q)
        k = jax.nn.silu(k)
        q = _lrpe(q, theta, n)
        k = _lrpe(k, theta, n)
        tril = jnp.tril(jnp.ones((n, n), dtype=x.dtype))
        mask = jnp.exp(slope_rate * tril)
        energy = jnp.einsum('bhne,bhme->bhnm', q, k) * mask[None]
        out = jnp.einsum('bhnm,bhmd->bhnd', energy, v)
        out = out.transpose(0, 2, 1, 3).reshape(b, n, hd)
        out = _srmsnorm(out)
        out = u * out
        out = out @ out_w.T + out_b
        return out

    def _L0_ffn_ref(x, wqkv, q_scale, k_scale, wo, ln_g, ln_b, w1, b1, w2, b2):
        import jax, jax.numpy as jnp
        import numpy as np
        DIM = 128
        DEPTH = 2
        HEADS = 8
        DIM_HEAD = 64
        WINDOW = 64
        INNER = HEADS * DIM_HEAD
        HID = int(DIM * 4 * 2 / 3)
        B, N = (2, 1024)
        QK_SCALE = 8.0

        def shift_token(t):
            t1, t2 = jnp.split(t, 2, axis=-1)
            t2 = jnp.pad(t2, ((0, 0), (1, 0), (0, 0)))[:, :-1]
            return jnp.concatenate([t1, t2], axis=-1)

        def l2norm(t):
            return t / jnp.clip(jnp.linalg.norm(t, axis=-1, keepdims=True), 1e-12)

        def rotate_half(x):
            x1, x2 = jnp.split(x, 2, axis=-1)
            return jnp.concatenate([-x2, x1], axis=-1)

        def rotary_xpos(q, k):
            n = q.shape[-2]
            half_idx = jnp.arange(0, DIM_HEAD, 2, dtype=jnp.float32)
            inv_freq = 1.0 / 10000.0 ** (half_idx / DIM_HEAD)
            t = jnp.arange(n, dtype=jnp.float32)
            freqs = t[:, None] * inv_freq[None, :]
            freqs = jnp.concatenate([freqs, freqs], axis=-1)
            base = (half_idx + 0.4 * DIM_HEAD) / (1.4 * DIM_HEAD)
            power = (t - n // 2) / float(WINDOW // 2)
            scale = base[None, :] ** power[:, None]
            scale = jnp.concatenate([scale, scale], axis=-1)
            cos, sin = (jnp.cos(freqs), jnp.sin(freqs))
            q = q * cos * scale + rotate_half(q) * sin * scale
            k = k * cos / scale + rotate_half(k) * sin / scale
            return (q, k)

        def local_attention(q, k, v):
            b, h, n, d = q.shape
            w = n // WINDOW
            bq = q.reshape(b, h, w, WINDOW, d) * QK_SCALE
            bk = k.reshape(b, h, w, WINDOW, d)
            bv = v.reshape(b, h, w, WINDOW, d)

            def look_around(t):
                p = jnp.pad(t, ((0, 0), (0, 0), (1, 0), (0, 0), (0, 0)))
                return jnp.concatenate([p[:, :, :w], p[:, :, 1:]], axis=3)
            bk, bv = (look_around(bk), look_around(bv))
            bt = jnp.arange(n).reshape(w, WINDOW)
            btp = jnp.pad(bt, ((1, 0), (0, 0)), constant_values=-1)
            btk = jnp.concatenate([btp[:w], btp[1:]], axis=1)
            sim = jnp.einsum('bhwid,bhwjd->bhwij', bq, bk)
            i = bt[:, :, None]
            j = btk[:, None, :]
            mask = (i < j) | (i > j + WINDOW) | (j == -1)
            sim = jnp.where(mask, -jnp.finfo(sim.dtype).max, sim)
            attn = jax.nn.softmax(sim, axis=-1)
            out = jnp.einsum('bhwij,bhwjd->bhwid', attn, bv)
            return out.reshape(b, h, n, d)

        def _layer(x, wqkv, qs, ksc, wo, lg, lb, w1, b1, w2, b2):
            b, n, _ = x.shape
            h = shift_token(x)
            qkv = h @ wqkv
            q, k, v = jnp.split(qkv, 3, axis=-1)
            to_heads = lambda t: t.reshape(b, n, HEADS, DIM_HEAD).transpose(0, 2, 1, 3)
            q, k, v = (to_heads(q), to_heads(k), to_heads(v))
            q = l2norm(q) * qs
            k = l2norm(k) * ksc
            q, k = rotary_xpos(q, k)
            o = local_attention(q, k, v)
            o = o.transpose(0, 2, 1, 3).reshape(b, n, INNER)
            x = x + o @ wo
            h = shift_token(x)
            mu = h.mean(-1, keepdims=True)
            var = h.var(-1, keepdims=True)
            h = (h - mu) / jnp.sqrt(var + 1e-05) * lg + lb
            h = h @ w1 + b1
            a, g = jnp.split(h, 2, axis=-1)
            h = a * jax.nn.gelu(g, approximate=False)
            x = x + h @ w2 + b2
            return x
        for l in range(DEPTH):
            x = _layer(x, wqkv[l], q_scale[l], k_scale[l], wo[l], ln_g[l], ln_b[l], w1[l], b1[l], w2[l], b2[l])
        return x

    def _L1_attn_ref(x, wave_w, wave_b, kernel_w, kernel_b, out_w):
        import jax, jax.numpy as jnp
        import numpy as np
        B, L, C = (4, 128, 128)
        H = 8
        D = C // H
        MAX_SAMPLES = 32
        HALF_S = MAX_SAMPLES // 2
        S = 2 * HALF_S + 1
        K = 64
        MAX_FREQ = 16.0
        MIN_FREQ = 1.0

        def _silu(v):
            return v * jax.nn.sigmoid(v)
        Bb, Ll, Cc = x.shape
        wave = _silu(x @ wave_w.T + wave_b).reshape(Bb, Ll, 2, H)
        freq = jax.nn.sigmoid(wave[:, :, 0, :]) * (MAX_FREQ - MIN_FREQ) + MIN_FREQ
        phase = jnp.tanh(wave[:, :, 1, :]) * MAX_FREQ
        freq_avg = freq.mean(axis=-1)
        phase_avg = phase.mean(axis=-1)
        kernel = _silu(x @ kernel_w.T + kernel_b).reshape(Bb, Ll, H, K)
        w = kernel[:, :, :, :S]
        s_idx = jnp.arange(S, dtype=x.dtype) - HALF_S
        base = jnp.arange(Ll, dtype=x.dtype)
        pos = base[None, :, None] + s_idx[None, None, :] * freq_avg[:, :, None] + phase_avg[:, :, None]
        pos = jnp.clip(pos, 0.0, Ll - 1.0)
        lo = jnp.floor(pos).astype(jnp.int32)
        hi = jnp.minimum(lo + 1, Ll - 1)
        frac = pos - lo.astype(x.dtype)
        xh = x.reshape(Bb, Ll, H, D)
        b_ix = jnp.arange(Bb)[:, None, None]
        g_lo = xh[b_ix, lo]
        g_hi = xh[b_ix, hi]
        g = g_lo + frac[..., None, None] * (g_hi - g_lo)
        out_h = jnp.einsum('blshd,blhs->blhd', g, w)
        out = out_h.reshape(Bb, Ll, Cc)
        return _silu(out @ out_w.T)

    def _L1_ffn_ref(x, gate_w, gate_b, w1, b1, w2, b2, w3, b3):
        import jax, jax.numpy as jnp
        import numpy as np
        K = 2
        E = gate_w.shape[-1]
        logits = jnp.einsum('bsd,de->bse', x, gate_w) + gate_b
        probs = jax.nn.softmax(logits, axis=1)
        vals, idx = jax.lax.top_k(probs, K)
        h = jax.nn.relu(jnp.einsum('bsd,edo->ebso', x, w1) + b1[:, None, None, :])
        h = jax.nn.relu(jnp.einsum('ebso,eop->ebsp', h, w2) + b2[:, None, None, :])
        y = jax.nn.relu(jnp.einsum('ebso,eop->ebsp', h, w3) + b3[:, None, None, :])
        onehot = jax.nn.one_hot(idx, E, dtype=x.dtype)
        w_tok = jnp.einsum('bske,bsk->bse', onehot, vals)
        ind = onehot.max(axis=2)
        v = jnp.einsum('ebso,bse->eo', y, w_tok)
        out = jnp.einsum('bse,eo->bso', ind, v)
        return out
    x = L0_attn_x
    x = _layernorm(x + _L0_attn_ref(x, L0_attn_slope_rate, L0_attn_qkvu_w, L0_attn_qkvu_b, L0_attn_out_w, L0_attn_out_b, L0_attn_theta), axis=-1)
    x = _layernorm(x + _L0_ffn_ref(x, L0_ffn_wqkv, L0_ffn_q_scale, L0_ffn_k_scale, L0_ffn_wo, L0_ffn_ln_g, L0_ffn_ln_b, L0_ffn_w1, L0_ffn_b1, L0_ffn_w2, L0_ffn_b2), axis=-1)
    x = _layernorm(x + _L1_attn_ref(x, L1_attn_wave_w, L1_attn_wave_b, L1_attn_kernel_w, L1_attn_kernel_b, L1_attn_out_w), axis=-1)
    x = _layernorm(x + _L1_ffn_ref(x, L1_ffn_gate_w, L1_ffn_gate_b, L1_ffn_w1, L1_ffn_b1, L1_ffn_w2, L1_ffn_b2, L1_ffn_w3, L1_ffn_b3), axis=-1)
    return x

_drawn_inputs = setup_inputs


def setup_inputs(seed=0):
    import zlib

    import numpy as np

    out = dict(_drawn_inputs(seed))
    spreads = {'L0_attn_qkvu_b': (0.0, 0.1),
     'L0_attn_out_b': (0.0, 0.1),
     'L0_ffn_q_scale': (1.0, 0.6),
     'L0_ffn_k_scale': (1.0, 0.6),
     'L0_ffn_ln_g': (1.0, 0.6),
     'L0_ffn_ln_b': (0.0, 0.8),
     'L0_ffn_b1': (0.0, 0.8),
     'L0_ffn_b2': (0.0, 0.1),
     'L1_attn_wave_b': (0.0, 0.8),
     'L1_attn_kernel_b': (0.0, 0.654)}
    factors = {'L0_attn_slope_rate': 8.0,
     'L0_ffn_wqkv': 3.729,
     'L0_ffn_wo': 3.626,
     'L0_ffn_w1': 6.084,
     'L0_ffn_w2': 6.029,
     'L1_attn_wave_w': 4.252,
     'L1_attn_kernel_w': 4.689,
     'L1_attn_out_w': 3.298,
     'L1_ffn_gate_w': 3.011,
     'L1_ffn_gate_b': 8.0,
     'L1_ffn_w1': 8.0,
     'L1_ffn_b1': 8.0,
     'L1_ffn_w2': 8.0,
     'L1_ffn_b2': 8.0,
     'L1_ffn_w3': 8.0,
     'L1_ffn_b3': 2.726}
    for name, (base, spread) in spreads.items():
        noise = np.random.default_rng([zlib.crc32(name.encode()), seed]).standard_normal(out[name].shape)
        drawn = base * np.exp(spread * noise) if base else spread * noise
        out[name] = jnp.asarray(drawn.astype(out[name].dtype))
    for name, factor in factors.items():
        out[name] = (out[name] * factor).astype(out[name].dtype)
    return out
```

```python
from contextlib import ExitStack

import concourse.bass as bass
from concourse import mybir

F32 = mybir.dt.float32
BF16 = mybir.dt.bfloat16
I32 = mybir.dt.int32
U32 = mybir.dt.uint32
ALU = mybir.AluOpType
ACT = mybir.ActivationFunctionType
AXX = mybir.AxisListType.X

P = 128
B, N, D = 4, 1024, 128
T = N // P
BLK = 512
J = N // BLK
TB = BLK // P
LN_EPS = 1e-5

H, HD = 8, 16
G = 2
RMS_EPS = 1e-6
TWO_PI_HI, TWO_PI_MID, TWO_PI_LO = 6.28125, 0.0019350051879882812, 3.0199159819e-07
PI_IN = 3.1415925
ROUND = 12582912.0

LAYERS, HB, DH, WIN = 2, 8, 64, 64
INNER = HB * DH
PAIRS = HB // 2
HID = int(D * 4 * 2 / 3)
FB = -(-HID // P)
FW = [min(P, HID - P * i) for i in range(FB)]
KEYS = WIN + P
MASKED = -1e30
UNITS = 2 * T

S, KS = 33, 64
CW = 2 * H + H * S
SC = 11
NC_ = S // SC
GB = 3

E_ = 8


def ap3(tensor_ap, dims):
    return bass.AP(tensor=tensor_ap.tensor, offset=tensor_ap.offset, ap=[tensor_ap.ap[0]] + [list(d) for d in dims])


def plan(keys):
    where, turns, nxt = {}, {}, {}
    for key, pool in keys:
        i = nxt.get(pool, 0)
        bank = pool[i % len(pool)]
        nxt[pool] = i + 1
        where[key] = (bank, turns.get(bank, 0))
        turns[bank] = turns.get(bank, 0) + 1
    return where, turns


PROJ, SCORE, TURN, CB = ("pa", "pb"), ("sc",), ("ta", "tb"), ("c0", "c1")


def ln_keys(m):
    return [(("mean", m), PROJ), (("var", m), PROJ)]


def attention_steps():
    steps = [("proj", 0), ("v", 0), ("turn", 0)]
    for n in range(UNITS + 1):
        t, g = divmod(n, 2)
        if n < UNITS:
            steps.append(("S", n))
        if g == 0 and t + 1 < T:
            steps.append(("proj", t + 1))
        if n >= 1:
            steps.append(("P", n - 1))
        if g == 1 and t + 1 < T:
            steps += [("v", t + 1), ("turn", t + 1)]
        if n >= 1:
            steps.append(("O", n - 1))
        if g == 1 and t >= 1:
            steps.append(("oT", t - 1))
            if t % TB == 0:
                steps.append(("wo", t // TB - 1))
    steps += [("oT", T - 1), ("wo", J - 1)]
    return steps


def ab_keys():
    k = [(("xT", j), PROJ) for j in range(J)]
    k += [((w, j, g), PROJ) for w in "kq" for j in range(J) for g in range(G)]
    k += [(("vu", p), PROJ) for p in range(T // 2)]
    k += [(("kt", p), TURN) for p in range(T // 2)]
    k += [(("KV", j), TURN) for j in range(J)]
    k += [(("E", p, r), (("pa", "pb", "ta", "tb")[r],)) for p in range(T // 2) for r in range(4)]
    k += [(("att",), SCORE)]
    k += [(("yT", j), PROJ) for j in range(J)] + [(("ao", j), PROJ) for j in range(J)]
    k += ln_keys(0) + ln_keys(1)
    for l in range(LAYERS):
        for what, n in attention_steps():
            if what == "proj":
                k += [(("qp", l, n), PROJ), (("kp", l, n), PROJ)]
            elif what == "v":
                k += [(("vp", l, n), PROJ)]
            elif what == "turn":
                k += [(("qT", l, n), TURN), (("kT", l, n), TURN)]
            elif what == "S":
                k += [(("S", l, n), SCORE)]
            elif what == "P":
                k += [(("Pc", l, n), TURN), (("Pp", l, n), TURN)]
            elif what == "O":
                k += [(("O", l, n), TURN)]
            elif what == "oT":
                k += [(("oT", l, n), TURN)]
            else:
                k += [(("wo", l, n), PROJ)]
        for j in range(J):
            k += ln_keys(2 + 2 * l + j)
            for f in range(FB):
                k += [(("gate", l, j, f), PROJ), (("up", l, j, f), PROJ)]
            k += [(("down", l, j), PROJ)]
    k += ln_keys(6) + ln_keys(7)
    return k


def moe_steps():
    out = []
    for q in range(2 * E_ + 3):
        for what, lag in (("h1", 0), ("h2", 1), ("y", 2), ("vs", 3)):
            if 0 <= q - lag < 2 * E_:
                out.append((what, q - lag))
    return out


def cd_keys():
    k = [(("x2t", j), CB) for j in range(J)] + [(("wk", t), CB) for t in range(T)]
    for t in range(T):
        k += [(("sum", t), CB)]
        if t % TB == TB - 1:
            k += [(("cT", t // TB), CB), (("co", t // TB), CB)]
    k += [(("x3T", j), CB) for j in range(J)] + [(("lg", j), CB) for j in range(J)]
    k += [(("pT",), CB)] + [(("iT", j), CB) for j in range(J)]
    k += [((what, q), CB) for what, q in moe_steps()]
    return k


def build(nc, A):
    ab_where, ab_turns = plan(ab_keys())
    cd_where, cd_turns = plan(cd_keys())
    where = {**ab_where, **cd_where}
    turns = {**ab_turns, **cd_turns}

    with ExitStack() as ctx:
        def sb(name, shape, dt=F32):
            return ctx.enter_context(nc.sbuf_tensor(name, shape, dt))

        psum = {n: ctx.enter_context(nc.psum_tensor(n, [P, BLK], F32)) for n in ("pa", "pb", "ta", "tb", "c0", "c1")}
        psum["sc"] = ctx.enter_context(nc.psum_tensor("sc", [P, 2, BLK], F32))

        wkq = sb("wkq", [P, 2, G * P])
        wvu = sb("wvu", [P, 2 * D])
        ow1 = sb("ow1", [P, D])
        wqkv = sb("wqkv", [P, LAYERS, 3 * INNER])
        wo = sb("wo", [P, LAYERS, 4, D])
        w1 = sb("w1", [P, LAYERS, 2 * HID])
        w2 = sb("w2", [P, LAYERS, FB, D])
        wc = sb("wc", [P, CW])
        ow2 = sb("ow2", [P, D])
        gw = sb("gw", [P, E_])
        m1 = sb("m1", [P, E_, D])
        m2 = sb("m2", [P, E_, D])
        m3 = sb("m3", [P, E_, D])
        kqb = sb("kqb", [P, 2, G])
        vub = sb("vub", [P, 2 * D])
        cols = sb("cols", [P, 64])
        ident = sb("ident", [P, P])
        identb = sb("identb", [P, P], BF16)
        meanw = sb("meanw", [P, P])
        blockd = sb("blockd", [P, D // G])
        band = sb("band", [P, 2, KEYS], BF16)
        emask = sb("emask", [P, 4, G, P])
        es = sb("es", [P, G])
        csT = sb("csT", [P, G, N])
        rot = sb("rot", [P, LAYERS, T, 2, 2, DH])
        cb = sb("cb", [P, CW])
        sidx = sb("sidx", [P, S])
        base = sb("base", [P, T])
        b3 = sb("b3", [P, E_ * D])
        ties = sb("ties", [P, E_, E_])
        half = sb("half", [P, 16])
        gb = sb("gb", [E_, 1])
        slope = sb("slope", [P, H])
        slope_c = sb("slope_c", [P, G])
        OB, LG, LB, BG, BA, B2, C1, C2, TH, PH, EPS, REPS = 0, 1, 3, 5, 11, 17, 19, 27, 35, 37, 38, 39

        def col(i, rows=P):
            return cols[0:rows, i:i + 1]

        x1 = sb("x1", [P, 1 + N])
        xb = sb("xb", [P, 1 + N])
        xm = sb("xm", [P, 1 + N])
        x2 = xm[:, 1:1 + N]
        x2tok = sb("x2tok", [P, T, D])
        z = x2tok[:].rearrange("p t d -> p (t d)").rearrange("p (j c) -> p j c", j=J)
        lnc = sb("lnc", [P, 2, BLK])
        lnq = sb("lnq", [P, 2, BLK])
        keyT = sb("keyT", [P, PAIRS, WIN + N])
        vring = sb("vring", [P, 4, HB, DH + 1])
        prob = sb("prob", [P, 2, 4, 2 * P])
        pool_a = sb("pool_a", [P, 15296])
        used = {"a": 0, "b": 0, "c": 0}

        def part(which, *shape):
            n = 1
            for s in shape:
                n *= s
            at = used[which]
            used[which] = at + n
            v = pool_a[:, at:at + n]
            if len(shape) == 1:
                return v
            names = " ".join(f"d{i}" for i in range(len(shape)))
            return v.rearrange(f"p ({names}) -> p {names}", **{f"d{i}": s for i, s in enumerate(shape)})

        keyA = part("a", G, N)
        qryA = part("a", G, N)
        silu4 = part("a", 4, BLK)
        ktok = silu4.rearrange("p a (b c) -> p (a b) c", b=2)
        KV = part("a", T, D)
        pre = part("a", T, D)
        suf = part("a", T, D)
        st = part("a", T, D)
        vu = part("a", T, 2 * D)
        em0 = part("a", 4, BLK)
        y = KV
        yT = pre.rearrange("p a b -> p (a b)")
        xtok = sb("xtok", [P, T, D])
        ss1 = sb("ss1", [P, 3, T])
        hT = part("b", N)
        sq = part("b", 2, BLK)
        qn = part("b", 2, HB, DH)
        r1 = part("b", 2, HB, DH)
        r2 = part("b", 2, HB, DH)
        qk = part("b", 2, 2, INNER)
        qTs = part("b", 2, PAIRS, P)
        PTc = part("b", 2, 4, P)
        PTp = part("b", 2, 4, WIN)
        oS = part("b", 2, INNER)
        oT = part("b", 4, BLK)
        h2 = sb("h2", [P, BLK])
        hn = h2
        gel = sq
        up = part("b", FB, BLK) if False else qk.rearrange("p a b c -> p (a b c)")[:, 0:FB * BLK].rearrange("p (f c) -> p f c", f=FB)
        ssq = sb("ssq", [P, 2, 3, 16])
        nmax = sb("nmax", [P, 2, 4])
        rsum = sb("rsum", [P, 2, 4])
        wk = part("c", T, CW)
        sgt = part("c", 2, T, H)
        fp = part("c", 4, T)
        pos = part("c", T, S)
        lo = part("c", T, S)
        tmp = part("c", T, S)
        frac = part("c", T * S, 2)
        idx = sb("idx", [P, T, S], U32)
        wlh = part("c", 2, S, 2, H)
        gat = part("c", GB, SC, 2 * D)
        osum = part("c", T, D)
        cT = part("c", BLK)
        zc = part("c", TB, D)
        bn = sb("bn", [P, T, 6])
        mv = sb("mv", [P, T, 2])
        rst = sb("rst", [P, 2, T])
        x3 = x2tok
        x3T = wk.rearrange("p a b -> p (a b)")[:, 0:N]
        lgs = sb("lgs", [E_, 3])
        prT = sb("prT", [P, T, E_])
        gf = gat.rearrange("p a b c -> p (a b c)")
        lgS = gf[0:E_, 5120:5120 + N]
        rk1 = gf[:, 0:512].rearrange("p (t e f) -> p t e f", t=T, e=E_)
        rk2 = gf[:, 512:1024].rearrange("p (t e f) -> p t e f", t=T, e=E_)
        cnt = sb("cnt", [P, T * E_])
        ind = sb("ind", [P, T * E_])
        wt = sb("wt", [P, T, E_])
        indT = pool_a[0:E_, 0:B * N]
        h1s = gf[:, 1024:2048].rearrange("p (a b) -> p a b", a=2)
        h2s = gf[:, 2048:3072].rearrange("p (a b) -> p a b", a=2)
        ys = gf[:, 3072:5120].rearrange("p (a b) -> p a b", a=4)
        vacc = sb("vacc", [P, E_])
        v8 = sb("v8", [E_, D])
        assert max(used.values()) <= 15296, used
        posr = pool_a[:, 0:N]
        ang = pool_a[:, N:3 * N].rearrange("p (g n) -> p g n", g=G)
        kk = pool_a[:, 3 * N:5 * N].rearrange("p (g n) -> p g n", g=G)
        rbase = pool_a[:, 5 * N:7 * N].rearrange("p (t c) -> p t c", t=T)
        qkscale = pool_a[:, 7 * N:7 * N + 512].rearrange("p (l c) -> p l c", l=LAYERS)
        tri = pool_a[:, 8 * N:8 * N + P]

        table = nc.dram_tensor("rows_of_x2", (N + 1, 2 * D), F32, kind="Internal").ap()
        ind_dram = nc.dram_tensor("chosen_experts", (B, E_, N), F32, kind="Internal").ap()
        x3_dram = nc.dram_tensor("x3_of_all", (B * N, D), F32, kind="Internal").ap()

        PER = {
            "x_loaded": 16, "a_rot": 8, "a_scan": 16, "a_state": 2, "a_square": 8, "a_rstd": 2, "a_y": 8,
            "ln_square": 8, "ln_log": 8, "ln_rstd": 8, "ln_out": 8,
            "b_shift": 8, "b_square": 32, "b_ss": 16, "b_rn": 32, "b_cos": 16, "b_sin": 32, "b_qk": 16,
            "b_max": 32, "b_recip": 32, "f_shift": 8, "f_hn": 4, "f_res": 2,
            "c_silu": 1, "c_act": 2, "c_pos": 13, "c_w": 8, "c_table": 64, **{f"c_gather{i}": 16 * S * T // GB for i in range(GB)}, "c_prod": 24, "c_read": 16,
            "c_z": 2, "c_bn": 16, "c_rstd": 4, "c_x3": 8, "c_saved": 32,
            "d_max": 3, "d_exp": 1, "d_rank": 7, "d_relu": 16,
        }
        SEM = {n: ctx.enter_context(nc.semaphore(n)) for n in PER}
        filled = {n: ctx.enter_context(nc.semaphore(f"{n}_filled")) for n in psum}
        drained = {n: ctx.enter_context(nc.semaphore(f"{n}_drained")) for n in psum}
        loaded = ctx.enter_context(nc.semaphore("weights_loaded"))
        setup = {n: ctx.enter_context(nc.semaphore(f"setup_{n}")) for n in ("dve", "act", "pool")}
        last = {n: ctx.enter_context(nc.semaphore(f"final_{n}")) for n in ("filled", "drained", "vt", "x0", "x1", "bn", "pool", "out", "stored0", "stored1", "z", "ind")}

        def reach(eng, sem, value):
            if not isinstance(value, int) or value > 0:
                eng.wait_ge(sem, value)
                if not isinstance(value, int) and eng in (nc.gpsimd, nc.sync):
                    apart(eng)

        def apart(eng):
            eng.nop(nofuse=True)

        def wait(eng, name, b, n):
            reach(eng, SEM[name], b * PER[name] + n)

        def wait_filled(eng, key, b):
            bank, n = where[key]
            reach(eng, filled[bank], b * turns[bank] + n + 1)
            return psum[bank]

        def wait_drained(eng, key, b):
            bank, n = where[key]
            reach(eng, drained[bank], b * turns[bank] + n + 1)

        def wait_free(eng, key, b):
            bank, n = where[key]
            reach(eng, drained[bank], b * turns[bank] + n)
            return psum[bank]

        def full(key):
            return filled[where[key][0]]

        def empty(key):
            return drained[where[key][0]]

        weight_loads = A["loads"](locals())
        n_loads = len(weight_loads)

        block = ctx.enter_context(nc.Block())

        @block.sync
        def _(sp):
            def load_x(b):
                wait_drained(sp, ("xT", J - 1), b - 1)
                sp.dma_start(xtok[:], A["x"][b].rearrange("(t p) d -> p t d", p=P)).then_inc(SEM["x_loaded"], 16)

            def save_rows(b):
                wait_drained(sp, ("x2t", J - 1), b)
                for i in range(GB):
                    wait(sp, f"c_gather{i}", b, 0)
                rows = table[:, D:2 * D]
                sp.dma_start(table[1:N + 1, 0:D].rearrange("(t p) d -> p t d", p=P), x2tok[:]).then_inc(SEM["c_table"], 16)
                sp.dma_start(rows[0:N].rearrange("(t p) d -> p t d", p=P), x2tok[:]).then_inc(SEM["c_table"], 16)
                sp.dma_start(table[0:1, 0:D], x2tok[0:1, 0, :]).then_inc(SEM["c_table"], 16)
                sp.dma_start(rows[N:N + 1], x2tok[P - 1:P, T - 1, :]).then_inc(SEM["c_table"], 16)

            def save_x3(b):
                wait(sp, "c_x3", b, T)
                sp.dma_start(A["x3v"](x3_dram, b), x3[:]).then_inc(SEM["c_saved"], 16)
                wait_drained(sp, ("iT", J - 1), b)
                sp.dma_start(ind_dram[b], lgS).then_inc(SEM["c_saved"], 16)

            def batch(b):
                save_rows(b)
                save_x3(b)

            load_x(0)
            for dst, src in weight_loads:
                sp.dma_start(dst, src).then_inc(loaded, 16)
            batch(0)
            with sp.Fori(1, B) as b:
                load_x(b)
                batch(b)
            sp.wait_ge(SEM["c_saved"], 32 * B)
            sp.wait_ge(last["filled"], 1)
            sp.dma_start(indT.rearrange("e (b n) -> e b n", b=B), ind_dram.rearrange("b e n -> e b n")).then_inc(last["ind"], 16)
            for i in range(B * J):
                if i >= 2:
                    sp.wait_ge(last["z"], i - 1)
                sp.dma_start(x2tok[:, TB * (i % 2):TB * (i % 2) + TB, :],
                             x3_dram[BLK * i:BLK * i + BLK].rearrange("(t p) d -> p t d", p=P)).then_inc(last[f"x{i % 2}"], 16)
                if i >= 1:
                    sp.wait_ge(last["out"], TB * i)
                    sp.dma_start(A["outv"](i - 1), osum[:, TB * ((i - 1) % 2):TB * ((i - 1) % 2) + TB, :]).then_inc(last[f"stored{(i - 1) % 2}"], 16)
            sp.wait_ge(last["out"], TB * B * J)
            sp.dma_start(A["outv"](B * J - 1), osum[:, TB:2 * TB, :]).then_inc(last["stored1"], 16)
            sp.wait_ge(last["stored0"], 8 * B * J)
            sp.wait_ge(last["stored1"], 8 * B * J)

        @block.gpsimd
        def _(pool):
            nc.gpsimd.memset(half[:], -0.5)
            nc.gpsimd.memset(x1[:, 0:1], 0.0)
            nc.gpsimd.memset(xb[:, 0:1], 0.0)
            nc.gpsimd.memset(xm[:, 0:1], 0.0)
            nc.gpsimd.memset(keyT[:, :, 0:WIN], 0.0)
            nc.gpsimd.memset(prob[:], 0.0)
            nc.gpsimd.memset(vring[:], 1.0)
            nc.gpsimd.memset(vacc[:], 0.0)
            nc.gpsimd.memset(meanw[:], 1.0 / D).then_inc(setup["pool"], 1)
            pool.wait_ge(setup["pool"], 1)

            def first_attention(b):
                for i in range(8):
                    w, j, g = "kq"[i // 4], i % 4 // 2, i % 2
                    wait_drained(pool, (w, j, g), b)
                    dst = (keyA, qryA)[i // 4][:, g, BLK * j:BLK * (j + 1)]
                    nc.gpsimd.tensor_tensor(dst, silu4[:, i % 4, :], csT[:, g, BLK * j:BLK * (j + 1)], ALU.mult).then_inc(SEM["a_rot"], 1)
                wait_drained(pool, ("KV", J - 1), b)
                nc.gpsimd.memset(pre[:, 0, :], 0.0).then_inc(SEM["a_scan"], 1)
                nc.gpsimd.memset(suf[:, T - 1, :], 0.0).then_inc(SEM["a_scan"], 1)
                for t in range(1, T):
                    wait(pool, "a_scan", b, 2 * t)
                    u = T - 1 - t
                    nc.gpsimd.tensor_tensor(pre[:, t, :], pre[:, t - 1, :], KV[:, t - 1, :], ALU.add).then_inc(SEM["a_scan"], 1)
                    nc.gpsimd.tensor_tensor(suf[:, u, :], suf[:, u + 1, :], KV[:, u + 1, :], ALU.add).then_inc(SEM["a_scan"], 1)
                wait(pool, "a_square", b, T)
                nc.gpsimd.tensor_scalar(ss1[:, 1, :], ss1[:, 0, :], 1.0 / D, RMS_EPS, ALU.mult, ALU.add).then_inc(SEM["a_rstd"], 1)
                wait(pool, "a_rstd", b, 1)
                nc.gpsimd.tensor_tensor(ss1[:, 2, :], ss1[:, 1, :], half[:, 0:T], ALU.pow).then_inc(SEM["a_rstd"], 1)

            def layer(b, l):
                for t in range(T):
                    i = T * l + t
                    wait(pool, "b_ss", b, i + 1)
                    nc.gpsimd.tensor_scalar(ssq[:, t % 2, 1, :], ssq[:, t % 2, 0, :], 1e-24, None, ALU.max).then_inc(SEM["b_rn"], 1)
                    wait(pool, "b_rn", b, 2 * i + 1)
                    nc.gpsimd.tensor_tensor(ssq[:, t % 2, 2, :], ssq[:, t % 2, 1, :], half[:, 0:16], ALU.pow).then_inc(SEM["b_rn"], 1)
                    wait_drained(pool, ("kp", l, t), b)
                    for w in range(2):
                        tab = ap3(rot[:, l, t, 0, w, :], [[0, HB], [1, DH]])
                        ins = nc.gpsimd.tensor_tensor(r1[:, w], qn[:, w], tab, ALU.mult)
                    ins.then_inc(SEM["b_cos"], 1)

            def sampling(b):
                wait(pool, "c_pos", b, 13)
                for t in range(T):
                    if t >= 2:
                        wait(pool, "c_prod", b, NC_ * (t - 1))
                    for c in range(2):
                        ins = nc.gpsimd.tensor_tensor(
                            wlh[:, t % 2, :, c, :], ap3(wk[:, t, 2 * H:], [[1, S], [S, H]]),
                            ap3(frac[:, S * t:, c], [[2, S], [0, H]]), ALU.mult)
                    ins.then_inc(SEM["c_w"], 1)
                    if t == 0:
                        wait(pool, "c_table", b, 64)
                    for c in range(NC_):
                        n = NC_ * t + c
                        if n >= GB:
                            m = n - GB
                            if m % NC_ == NC_ - 1:
                                wait_filled(pool, ("sum", m // NC_), b)
                            else:
                                wait(pool, "c_read", b, 2 * (m // NC_) + m % NC_ + 1)
                        for s in range(SC):
                            pool.indirect_dma_start(
                                gat[:, n % GB, s, :], None, table,
                                bass.IndirectOffsetOnAxis(ap=idx[:, t, SC * c + s:SC * c + s + 1], axis=0),
                            ).then_inc(SEM[f"c_gather{n % GB}"], 16)
                    if t % TB == 0 and t:
                        by_token_rstd(b, t // TB - 1)
                by_token_rstd(b, J - 1)

            def by_token_rstd(b, j):
                ts = slice(TB * j, TB * j + TB)
                wait(pool, "c_bn", b, T * (j + 1))
                nc.gpsimd.tensor_scalar(rst[:, 0, ts], mv[:, ts, 1], LN_EPS, None, ALU.add).then_inc(SEM["c_rstd"], 1)
                wait(pool, "c_rstd", b, 2 * j + 1)
                nc.gpsimd.tensor_tensor(rst[:, 1, ts], rst[:, 0, ts], half[:, 0:TB], ALU.pow).then_inc(SEM["c_rstd"], 1)

            def experts(b):
                for q in range(2 * E_):
                    wait_drained(pool, ("y", q), b)
                    nc.gpsimd.tensor_scalar(ys[:, q % 4, :], ys[:, q % 4, :], 0.0, None, ALU.max).then_inc(SEM["d_relu"], 1)

            def batch(b):
                first_attention(b)
                for l in range(LAYERS):
                    layer(b, l)
                sampling(b)
                experts(b)

            batch(0)
            with pool.Fori(1, B) as b:
                batch(b)
            for i in range(B * J):
                o = TB * (i % 2)
                pool.wait_ge(last["bn"], 2 * TB * (i + 1))
                nc.gpsimd.tensor_scalar(rst[:, 0, o:o + TB], mv[:, o:o + TB, 1], LN_EPS, None, ALU.add).then_inc(last["pool"], 1)
                pool.wait_ge(last["pool"], 2 * i + 1)
                nc.gpsimd.tensor_tensor(rst[:, 1, o:o + TB], rst[:, 0, o:o + TB], half[:, 0:TB], ALU.pow).then_inc(last["pool"], 1)

        @block.scalar
        def _(act):
            act.wait_ge(loaded, 16 * n_loads)
            for h in range(H):
                nc.scalar.activation(emask[:, h % 4, h // 4, :], tri, ACT.Exp, scale=slope[:, h:h + 1])
            nc.scalar.activation(es[:], slope_c[:], ACT.Exp)
            act.wait_ge(setup["dve"], 8)
            for g in range(G):
                nc.scalar.activation(csT[:, g, :], ang[:, g, :], ACT.Sin).then_inc(setup["act"], 1)

            def copy_out(key, dst, b, view=None):
                src = wait_filled(act, key, b)
                nc.scalar.copy(dst, src[:, :] if view is None else view(src)).then_inc(empty(key), 1)

            def first_attention(b):
                wait(act, "c_saved", b, 0)
                for j in range(J):
                    copy_out(("xT", j), xb[:, 1 + BLK * j:1 + BLK * (j + 1)], b)
                for i in range(8):
                    w, j, g = "kq"[i // 4], i % 4 // 2, i % 2
                    src = wait_filled(act, (w, j, g), b)
                    wait(act, "a_rot", b, i - 3)
                    nc.scalar.activation(silu4[:, i % 4, :], src[:, :], ACT.Silu, bias=kqb[:, i // 4, g:g + 1]).then_inc(empty((w, j, g)), 1)
                wait(act, "a_rot", b, 8)
                for p in range(T // 2):
                    copy_out(("kt", p), silu4[:, p, :], b)
                att = wait_filled(act, ("att",), b)
                for t in range(T):
                    nc.scalar.activation(yT[:, P * t:P * (t + 1)], att[:, t // TB, P * (t % TB):P * (t % TB + 1)], ACT.Square,
                                         accum_out=ss1[:, 0, t:t + 1]).then_inc(SEM["a_square"], 1)
                for j in range(J):
                    copy_out(("yT", j), yT[:, BLK * j:BLK * (j + 1)], b)
                for j in range(J):
                    layer_norm(b, j)

            def layer_norm(b, m):
                wait_drained(act, ("mean", m), b)
                nc.scalar.activation(lnq[:, m % 2, :], lnc[:, m % 2, :], ACT.Square).then_inc(SEM["ln_square"], 1)
                src = wait_filled(act, ("var", m), b)
                nc.scalar.activation(lnq[:, m % 2, :], src[:, :], ACT.Ln, bias=col(EPS)).then_inc(empty(("var", m)), 1)
                wait_drained(act, ("var", m), b)
                nc.scalar.activation(lnq[:, m % 2, :], lnq[:, m % 2, :], ACT.Exp, scale=-0.5).then_inc(SEM["ln_rstd"], 1)

            def unit(b, l, n):
                sc = wait_filled(act, ("S", l, n), b)
                wait(act, "b_max", b, UNITS * l + n + 1)
                for i in range(4):
                    ins = nc.scalar.activation(prob[:, n % 2, i, WIN:WIN + KEYS], sc[:, i // 2, KEYS * (i % 2):KEYS * (i % 2 + 1)],
                                               ACT.Exp, bias=nmax[:, n % 2, i:i + 1])
                ins.then_inc(empty(("S", l, n)), 1)

            def layer(b, l):
                for what, n in attention_steps():
                    if what == "proj":
                        wait(act, "b_ss", b, T * l + n)
                        for w, key in enumerate((("qp", l, n), ("kp", l, n))):
                            src = wait_filled(act, key, b)
                            nc.scalar.activation(sq[:, w, :], src[:, :], ACT.Square).then_inc(SEM["b_square"], 1)
                    elif what == "v":
                        copy_out(("vp", l, n), vring[:, n % 4, :, 0:DH], b, lambda s: s[:, :].rearrange("p (h d) -> p h d", h=HB))
                    elif what == "turn":
                        copy_out(("qT", l, n), qTs[:, n % 2], b, lambda s: s[:, :].rearrange("p (a b) -> p a b", a=PAIRS))
                        copy_out(("kT", l, n), keyT[:, :, WIN + P * n:WIN + P * (n + 1)], b, lambda s: s[:, :].rearrange("p (a b) -> p a b", a=PAIRS))
                    elif what == "S":
                        unit(b, l, n)
                    elif what == "P":
                        copy_out(("Pp", l, n), PTp[:, n % 2], b, lambda s: s[:, 0:4 * WIN].rearrange("p (a b) -> p a b", a=4))
                    elif what == "oT":
                        if n % TB == 0 and n:
                            wait_filled(act, ("wo", l, n // TB - 1), b)
                        copy_out(("oT", l, n), oT[:, :, P * (n % TB):P * (n % TB + 1)], b, lambda s: s[:, :].rearrange("p (a b) -> p a b", a=4))
                for j in range(J):
                    m = 2 + 2 * l + j
                    layer_norm(b, m)
                    wait(act, "ln_out", b, m + 1)
                    nc.scalar.activation(hn[:, :], lnc[:, m % 2, :], ACT.Identity, bias=col(LB + l)).then_inc(SEM["f_hn"], 1)
                    for f in range(FB):
                        w, key = FW[f], ("gate", l, j, f)
                        src = wait_filled(act, key, b)
                        if f >= 2:
                            wait_drained(act, ("up", l, j, f - 2), b)
                        nc.scalar.activation(gel[0:w, f % 2, :], src[0:w, :], ACT.Gelu, bias=col(BG + FB * l + f, w)).then_inc(empty(key), 1)

            def sampling(b):
                for j in range(J):
                    if j == 0:
                        wait(act, "c_saved", b, 0)
                    copy_out(("x2t", j), x2tok[:, TB * j:TB * (j + 1), :], b, lambda s: s[:, :].rearrange("p (a b) -> p a b", a=TB))
                wait_drained(act, ("wk", T - 1), b)
                nc.scalar.activation(wk[:], wk[:], ACT.Silu).then_inc(SEM["c_silu"], 1)
                wait(act, "c_silu", b, 1)
                nc.scalar.activation(sgt[:, 0], wk[:, :, 0:H], ACT.Sigmoid).then_inc(SEM["c_act"], 1)
                nc.scalar.activation(sgt[:, 1], wk[:, :, H:2 * H], ACT.Tanh).then_inc(SEM["c_act"], 1)
                for j in range(J):
                    copy_out(("cT", j), cT[:, :], b)
                    src = wait_filled(act, ("co", j), b)
                    wait(act, "c_x3", b, TB * j)
                    nc.scalar.activation(zc[:], src[:, :].rearrange("p (a b) -> p a b", a=TB), ACT.Silu).then_inc(empty(("co", j)), 1)

            def experts(b):
                for j in range(J):
                    copy_out(("x3T", j), x3T[:, BLK * j:BLK * (j + 1)], b)
                wait(act, "c_saved", b, 0)
                for j in range(J):
                    src = wait_filled(act, ("lg", j), b)
                    nc.scalar.activation(lgS[:, BLK * j:BLK * (j + 1)], src[0:E_, :], ACT.Identity, bias=gb[:]).then_inc(empty(("lg", j)), 1)
                wait(act, "d_max", b, 1)
                nc.scalar.activation(lgS, lgS, ACT.Exp, bias=lgs[:, 0:1], accum_out=lgs[:, 1:2]).then_inc(SEM["d_exp"], 1)
                for j in range(J):
                    copy_out(("iT", j), lgS[:, BLK * j:BLK * (j + 1)], b, lambda s: s[0:E_, :])
                for q in range(2 * E_):
                    key = ("h1", q)
                    src = wait_filled(act, key, b)
                    nc.scalar.activation(h1s[:, q % 2, :], src[:, :], ACT.Relu, bias=col(C1 + q // 2)).then_inc(empty(key), 1)

            def batch(b):
                first_attention(b)
                for l in range(LAYERS):
                    layer(b, l)
                for j in range(J):
                    layer_norm(b, 6 + j)
                sampling(b)
                experts(b)

            batch(0)
            with act.Fori(1, B) as b:
                batch(b)

        @block.vector
        def _(dve):
            V = nc.vector
            dve.wait_ge(loaded, 16 * n_loads)
            for g in range(G):
                V.tensor_scalar(ang[:, g, :], posr, col(TH + g), None, ALU.mult)
            V.tensor_copy(identb[:], ident[:]).then_inc(setup["dve"], 1)
            dve.wait_ge(setup["dve"], 1)
            V.tensor_scalar(kk[:, :, :], ang[:, :, :], col(PH), 0.15915494309189535, ALU.add, ALU.mult).then_inc(setup["dve"], 1)
            dve.wait_ge(setup["dve"], 2)
            V.tensor_scalar(kk[:, :, :], kk[:, :, :], ROUND, ROUND, ALU.add, ALU.subtract).then_inc(setup["dve"], 1)
            for i, part_of in enumerate((TWO_PI_HI, TWO_PI_MID, TWO_PI_LO)):
                dve.wait_ge(setup["dve"], 3 + i)
                V.scalar_tensor_tensor(ang[:, :, :], kk[:, :, :], -part_of, ang[:, :, :], ALU.mult, ALU.add).then_inc(setup["dve"], 1)
            dve.wait_ge(setup["dve"], 6)
            V.tensor_scalar(ang[:, :, :], ang[:, :, :], col(PH), PI_IN, ALU.add, ALU.min).then_inc(setup["dve"], 1)
            dve.wait_ge(setup["dve"], 7)
            for l in range(LAYERS):
                V.tensor_tensor(rot[:, l].rearrange("p t a b c -> p t (a b c)"), rbase,
                                ap3(qkscale[:, l, :], [[0, T], [1, 256]]), ALU.mult)
            V.tensor_scalar(ang[:, :, :], ang[:, :, :], -PI_IN, None, ALU.max).then_inc(setup["dve"], 1)

            def first_attention(b):
                wait(dve, "c_saved", b, 0)
                for p in range(T // 2):
                    src = wait_filled(dve, ("vu", p), b)
                    V.tensor_tensor(vu[:, 2 * p:2 * p + 2, :], src[:, :].rearrange("p (a b) -> p a b", a=2),
                                    ap3(vub[:], [[0, 2], [1, 2 * D]]), ALU.add).then_inc(empty(("vu", p)), 1)
                for j in range(J):
                    src = wait_filled(dve, ("KV", j), b)
                    V.tensor_tensor(KV[:, TB * j:TB * (j + 1), :].rearrange("p t (g c) -> p (t g) c", g=G),
                                    src[:, :].rearrange("p (a b) -> p a b", b=D // G),
                                    ap3(blockd[:], [[0, TB * G], [1, D // G]]), ALU.mult).then_inc(empty(("KV", j)), 1)
                wait(dve, "a_scan", b, 16)
                for g in range(G):
                    c = slice(64 * g, 64 * g + 64)
                    V.scalar_tensor_tensor(st[:, :, c], pre[:, :, c], es[:, g:g + 1], suf[:, :, c], ALU.mult, ALU.add).then_inc(SEM["a_state"], 1)
                for p in range(T // 2):
                    for r in range(4):
                        src = wait_filled(dve, ("E", p, r), b)
                        em = em0 if p % 2 else silu4
                        V.tensor_tensor(em[:, r, :].rearrange("p (t g c) -> p t g c", t=2, g=G),
                                        src[:, :].rearrange("p (t g c) -> p t g c", t=2, g=G),
                                        ap3(emask[:, r, :, :], [[0, 2], [P, G], [1, P]]), ALU.mult).then_inc(empty(("E", p, r)), 1)
                att = wait_filled(dve, ("att",), b)
                wait(dve, "a_rstd", b, 2)
                for t in range(T):
                    ins = V.scalar_tensor_tensor(y[:, t, :], att[:, t // TB, P * (t % TB):P * (t % TB + 1)], ss1[:, 2, t:t + 1],
                                                 vu[:, t, D:2 * D], ALU.mult, ALU.mult)
                ins.then_inc(empty(("att",)), 1)
                for j in range(J):
                    src = wait_filled(dve, ("ao", j), b)
                    V.scalar_tensor_tensor(z[:, j, :], src[:, :], col(OB), xb[:, 1 + BLK * j:1 + BLK * (j + 1)], ALU.add, ALU.add).then_inc(empty(("ao", j)), 1)
                for j in range(J):
                    layer_norm(b, j, z[:, j, :], x1[:, 1 + BLK * j:1 + BLK * (j + 1)])

            def layer_norm(b, m, src, dst, gamma=None):
                mean = wait_filled(dve, ("mean", m), b)
                V.tensor_tensor(lnc[:, m % 2, :], src, mean[:, :], ALU.subtract).then_inc(empty(("mean", m)), 1)
                wait(dve, "ln_rstd", b, m + 1)
                if gamma is None:
                    V.tensor_tensor(dst, lnc[:, m % 2, :], lnq[:, m % 2, :], ALU.mult).then_inc(SEM["ln_out"], 1)
                else:
                    V.scalar_tensor_tensor(dst, lnc[:, m % 2, :], gamma, lnq[:, m % 2, :], ALU.mult, ALU.mult).then_inc(SEM["ln_out"], 1)

            def shift(dst, src, j, sem):
                V.tensor_copy(dst[0:64], src[0:64, 1 + BLK * j:1 + BLK * (j + 1)]).then_inc(SEM[sem], 1)
                V.tensor_copy(dst[64:P], src[64:P, BLK * j:BLK * (j + 1)]).then_inc(SEM[sem], 1)

            def tile_qk(b, l, t):
                i = T * l + t
                wait(dve, "b_square", b, 2 * i + 2)
                V.tensor_reduce(ssq[:, t % 2, 0, :], sq[:, :, :].rearrange("p w (h d) -> p (w h) d", h=HB), AXX, ALU.add).then_inc(SEM["b_ss"], 1)
                wait(dve, "b_rn", b, 2 * i + 2)
                for w, key in enumerate((("qp", l, t), ("kp", l, t))):
                    src = wait_filled(dve, key, b)
                    V.tensor_tensor(qn[:, w], src[:, :].rearrange("p (h d) -> p h d", h=HB),
                                    ap3(ssq[:, t % 2, 2, HB * w:HB * (w + 1)], [[1, HB], [0, DH]]), ALU.mult).then_inc(empty(key), 1)
                wait_drained(dve, ("kp", l, t), b)
                for s in range(2):
                    a, o = 32 * s, 32 * (1 - s)
                    V.tensor_tensor(r2[:, :, :, a:a + 32], qn[:, :, :, o:o + 32],
                                    ap3(rot[:, l, t, 1, 0, a:], [[DH, 2], [0, HB], [1, 32]]), ALU.mult).then_inc(SEM["b_sin"], 1)
                wait(dve, "b_sin", b, 2 * i + 2)
                wait(dve, "b_cos", b, i + 1)
                V.tensor_tensor(qk[:, t % 2].rearrange("p w c -> p (w c)"), r1.rearrange("p w h d -> p (w h d)"),
                                r2.rearrange("p w h d -> p (w h d)"), ALU.add).then_inc(SEM["b_qk"], 1)

            def layer(b, l):
                x_in = (x1, xb)[l]
                for j in range(J):
                    if l == 0:
                        wait(dve, "ln_out", b, j + 1)
                    else:
                        wait_drained(dve, ("down", 0, j), b)
                    shift(hT[:, BLK * j:BLK * (j + 1)], x_in, j, "b_shift")
                for what, n in attention_steps():
                    if what == "proj":
                        tile_qk(b, l, n)
                    elif what == "S":
                        sc = wait_filled(dve, ("S", l, n), b)
                        V.tensor_reduce(nmax[:, n % 2, :], sc[:, :, 0:2 * KEYS].rearrange("p e (r k) -> p e r k", r=2), AXX, ALU.max,
                                        negate=True).then_inc(SEM["b_max"], 1)
                    elif what == "P":
                        src = wait_filled(dve, ("Pc", l, n), b)
                        V.tensor_copy(PTc[:, n % 2], src[:, :].rearrange("p (a b) -> p a b", a=4)).then_inc(empty(("Pc", l, n)), 1)
                    elif what == "O":
                        t, g = divmod(n, 2)
                        src = wait_filled(dve, ("O", l, n), b)[:, 0:4 * (DH + 1)].rearrange("p (i c) -> p i c", i=4)
                        V.reciprocal(rsum[:, n % 2, :], src[:, :, DH]).then_inc(SEM["b_recip"], 1)
                        wait(dve, "b_recip", b, UNITS * l + n + 1)
                        V.tensor_tensor(ap3(oS[:, t % 2, 256 * g:], [[DH, 2], [2 * DH, 2], [1, DH]]),
                                        src[:, :, 0:DH].rearrange("p (e r) c -> p e r c", e=2),
                                        ap3(rsum[:, n % 2, :], [[2, 2], [1, 2], [0, DH]]), ALU.mult).then_inc(empty(("O", l, n)), 1)
                    elif what == "wo":
                        src = wait_filled(dve, ("wo", l, n), b)
                        c = slice(1 + BLK * n, 1 + BLK * (n + 1))
                        V.tensor_tensor(xm[:, c], src[:, :], x_in[:, c], ALU.add).then_inc(empty(("wo", l, n)), 1)
                for j in range(J):
                    m, c = 2 + 2 * l + j, slice(1 + BLK * j, 1 + BLK * (j + 1))
                    wait_drained(dve, ("wo", l, j), b)
                    if l or j:
                        wait_drained(dve, ("up", l if j else l - 1, (j - 1) % 2, FB - 1), b)
                    shift(h2, xm, j, "f_shift")
                    wait(dve, "f_shift", b, 4 * l + 2 * j + 2)
                    layer_norm(b, m, h2[:, :], lnc[:, m % 2, :], col(LG + l))
                    for f in range(FB):
                        w, key = FW[f], ("up", l, j, f)
                        src = wait_filled(dve, key, b)
                        wait_drained(dve, ("gate", l, j, f), b)
                        V.scalar_tensor_tensor(up[0:w, f, :], src[0:w, :], col(BA + FB * l + f, w), gel[0:w, f % 2, :],
                                               ALU.add, ALU.mult).then_inc(empty(key), 1)
                    key = ("down", l, j)
                    src = wait_filled(dve, key, b)
                    dst = xb[:, c] if l == 0 else z[:, j, :]
                    V.scalar_tensor_tensor(dst, src[:, :], col(B2 + l), xm[:, c], ALU.add, ALU.add).then_inc(empty(key), 1)
                    if l == LAYERS - 1:
                        wait_drained(dve, key, b)
                        V.tensor_tensor(z[:, j, :], z[:, j, :], x1[:, c], ALU.add).then_inc(SEM["f_res"], 1)

            def sampling(b):
                for t in range(T):
                    src = wait_filled(dve, ("wk", t), b)
                    V.tensor_tensor(wk[:, t, :], src[:, 0:CW], cb[:], ALU.add).then_inc(empty(("wk", t)), 1)
                wait(dve, "c_act", b, 2)
                steps = [
                    lambda: V.tensor_reduce(fp[:, 0, :], sgt[:, 0], AXX, ALU.add),
                    lambda: V.tensor_reduce(fp[:, 1, :], sgt[:, 1], AXX, ALU.add),
                    lambda: V.tensor_scalar(fp[:, 2, :], fp[:, 0, :], 15.0 / H, 1.0, ALU.mult, ALU.add),
                    lambda: V.scalar_tensor_tensor(fp[:, 3, :], fp[:, 1, :], 16.0 / H, base[:], ALU.mult, ALU.add),
                    lambda: V.tensor_tensor(pos[:], ap3(sidx[:], [[0, T], [1, S]]), ap3(fp[:, 2, :], [[1, T], [0, S]]), ALU.mult),
                    lambda: V.tensor_tensor(pos[:], pos[:], ap3(fp[:, 3, :], [[1, T], [0, S]]), ALU.add),
                    lambda: V.tensor_scalar(pos[:], pos[:], 0.0, N - 1.0, ALU.max, ALU.min),
                    lambda: V.tensor_scalar(lo[:], pos[:], ROUND, ROUND, ALU.add, ALU.subtract),
                    lambda: V.tensor_tensor(tmp[:], lo[:], pos[:], ALU.is_gt),
                    lambda: V.tensor_tensor(lo[:], lo[:], tmp[:], ALU.subtract),
                    lambda: V.tensor_tensor(frac[:, :, 1].rearrange("p (t s) -> p t s", t=T), pos[:], lo[:], ALU.subtract),
                    lambda: V.tensor_scalar(frac[:, :, 0], frac[:, :, 1], -1.0, 1.0, ALU.mult, ALU.add),
                    lambda: V.tensor_scalar(idx[:], lo[:], 1.0, None, ALU.add),
                ]
                for i, step in enumerate(steps):
                    wait(dve, "c_pos", b, i)
                    step().then_inc(SEM["c_pos"], 1)
                for t in range(T):
                    wait(dve, "c_w", b, t + 1)
                    for c in range(NC_):
                        n = NC_ * t + c
                        wait(dve, f"c_gather{n % GB}", b, 16 * SC * (n // GB + 1))
                        g4 = gat[:, n % GB].rearrange("p s (c h d) -> p (s c) h d", c=2, h=H)
                        wv = ap3(wlh[:, t % 2, SC * c, 0, :], [[H, 2 * SC], [1, H], [0, HD]])
                        V.tensor_tensor(g4, g4, wv, ALU.mult).then_inc(SEM["c_prod"], 1)
                    src = wait_filled(dve, ("sum", t), b)
                    V.tensor_reduce(osum[:, t, :], ap3(src[:, 0:1], [[1, D], [D, 2]]), AXX, ALU.add).then_inc(empty(("sum", t)), 1)
                    if t % TB == TB - 1:
                        finish_block(b, t // TB)

            def finish_block(b, j):
                ts = slice(TB * j, TB * (j + 1))
                wait_drained(dve, ("co", j), b)
                V.tensor_tensor(zc[:], zc[:], x2tok[:, ts, :], ALU.add).then_inc(SEM["c_z"], 1)
                wait(dve, "c_z", b, j + 1)
                for t in range(TB * j, TB * (j + 1)):
                    V.bn_stats(bn[:, t, :], zc[:, t % TB, :]).then_inc(SEM["c_bn"], 1)
                wait(dve, "c_bn", b, T * j + TB)
                apart(dve)
                for t in range(TB * j, TB * (j + 1)):
                    V.bn_aggr(mv[:, t, :], bn[:, t, :]).then_inc(SEM["c_bn"], 1)
                wait(dve, "c_rstd", b, 2 * j + 2)
                if j == 0:
                    wait(dve, "c_table", b, 64)
                for t in range(TB * j, TB * (j + 1)):
                    V.tensor_scalar(x3[:, t, :], zc[:, t % TB, :], mv[:, t, 0:1], rst[:, 1, t:t + 1], ALU.subtract, ALU.mult).then_inc(SEM["c_x3"], 1)

            def experts(b):
                wait_drained(dve, ("lg", J - 1), b)
                V.tensor_reduce(lgs[:, 0:1], lgS, AXX, ALU.max, negate=True).then_inc(SEM["d_max"], 1)
                wait(dve, "d_exp", b, 1)
                V.reciprocal(lgs[:, 2:3], lgs[:, 1:2]).then_inc(SEM["d_max"], 1)
                wait(dve, "d_max", b, 2)
                V.tensor_scalar(lgS, lgS, lgs[:, 2:3], None, ALU.mult).then_inc(SEM["d_max"], 1)
                src = wait_filled(dve, ("pT",), b)
                V.tensor_copy(prT[:], src[:, 0:T * E_].rearrange("p (t e) -> p t e", t=T)).then_inc(empty(("pT",)), 1)
                wait_drained(dve, ("pT",), b)
                other = ap3(prT[:], [[E_, T], [0, E_], [1, E_]])
                own = ap3(prT[:], [[E_, T], [1, E_], [0, E_]])
                steps = [
                    lambda: V.tensor_tensor(rk1[:], other, own, ALU.is_gt),
                    lambda: V.tensor_tensor(rk2, other, own, ALU.is_equal),
                    lambda: V.tensor_tensor(rk2, rk2, ap3(ties[:], [[0, T], [E_, E_], [1, E_]]), ALU.mult),
                    lambda: V.tensor_tensor(rk1[:], rk1[:], rk2, ALU.add),
                    lambda: V.tensor_reduce(cnt[:], rk1[:].rearrange("p t e f -> p (t e) f"), AXX, ALU.add),
                    lambda: V.tensor_scalar(ind[:], cnt[:], 1.5, None, ALU.is_lt),
                    lambda: V.tensor_tensor(wt[:], ind[:].rearrange("p (t e) -> p t e", t=T), prT[:], ALU.mult),
                ]
                for i, step in enumerate(steps):
                    wait(dve, "d_rank", b, i)
                    step().then_inc(SEM["d_rank"], 1)
                for what, q in moe_steps():
                    if what == "h2":
                        src = wait_filled(dve, ("h2", q), b)
                        V.tensor_scalar(h2s[:, q % 2, :], src[:, :], col(C2 + q // 2), 0.0, ALU.add, ALU.max).then_inc(empty(("h2", q)), 1)
                    elif what == "y":
                        src = wait_filled(dve, ("y", q), b)
                        e = q // 2
                        V.tensor_tensor(ys[:, q % 4, :].rearrange("p (t c) -> p t c", t=TB), src[:, :].rearrange("p (t c) -> p t c", t=TB),
                                        ap3(b3[:, D * e:D * (e + 1)], [[0, TB], [1, D]]), ALU.add).then_inc(empty(("y", q)), 1)
                    elif what == "vs":
                        src = wait_filled(dve, ("vs", q), b)
                        if q >= 1:
                            wait_drained(dve, ("vs", q - 1), b)
                        V.tensor_tensor(vacc[:, q // 2:q // 2 + 1], vacc[:, q // 2:q // 2 + 1], src[:, 0:1], ALU.add).then_inc(empty(("vs", q)), 1)

            def batch(b):
                first_attention(b)
                for l in range(LAYERS):
                    layer(b, l)
                for j in range(J):
                    wait(dve, "f_res", b, j + 1)
                    layer_norm(b, 6 + j, z[:, j, :], x2[:, BLK * j:BLK * (j + 1)])
                sampling(b)
                experts(b)

            batch(0)
            with dve.Fori(1, B) as b:
                batch(b)
            dve.wait_ge(last["filled"], 1)
            V.tensor_copy(v8[:], psum["c0"][0:E_, 0:D]).then_inc(last["vt"], 1)
            for i in range(B * J):
                o = TB * (i % 2)
                dve.wait_ge(last["filled"], i + 2)
                dve.wait_ge(last[f"x{i % 2}"], 16 * (i // 2 + 1))
                xs = x2tok[:, o:o + TB, :]
                if i:
                    dve.wait_ge(last["out"], TB * i)
                V.tensor_tensor(zc[:], psum[CB[i % 2]][:, :].rearrange("p (a b) -> p a b", a=TB), xs, ALU.add).then_inc(last["z"], 1)
                dve.wait_ge(last["z"], i + 1)
                for t in range(TB):
                    V.bn_stats(bn[:, o + t, :], zc[:, t, :]).then_inc(last["bn"], 1)
                dve.wait_ge(last["bn"], 2 * TB * i + TB)
                for t in range(TB):
                    V.bn_aggr(mv[:, o + t, :], bn[:, o + t, :]).then_inc(last["bn"], 1)
                dve.wait_ge(last["pool"], 2 * i + 2)
                if i >= 2:
                    dve.wait_ge(last[f"stored{i % 2}"], 16 * (i // 2))
                for t in range(TB):
                    V.tensor_scalar(osum[:, o + t, :], zc[:, t, :], mv[:, o + t, 0:1], rst[:, 1, o + t:o + t + 1], ALU.subtract, ALU.mult).then_inc(last["out"], 1)

        @block.tensor
        def _(pe):
            pe.wait_ge(loaded, 16 * n_loads)
            pe.wait_ge(setup["pool"], 1)
            pe.wait_ge(setup["dve"], 1)
            PE = nc.tensor
            mm = PE.matmul

            def first_attention(b):
                wait(pe, "x_loaded", b, 16)
                for j in range(J):
                    out = wait_free(pe, ("xT", j), b)
                    for i in range(TB):
                        ins = PE.transpose(out[:, P * i:P * (i + 1)], xtok[:, TB * j + i, :], ident[:])
                    ins.then_inc(full(("xT", j)), 1)
                for w, name in enumerate("kq"):
                    for j in range(J):
                        wait_drained(pe, ("xT", j), b)
                        for g in range(G):
                            out = wait_free(pe, (name, j, g), b)
                            mm(out[:, :], wkq[:, w, P * g:P * (g + 1)], xb[:, 1 + BLK * j:1 + BLK * (j + 1)],
                               start=True, stop=True).then_inc(full((name, j, g)), 1)
                for p in range(T // 2):
                    out = wait_free(pe, ("vu", p), b)
                    for i in range(2):
                        t = 2 * p + i
                        ins = mm(out[:, 2 * D * i:2 * D * (i + 1)], xb[:, 1 + P * t:1 + P * (t + 1)], wvu[:], start=True, stop=True)
                    ins.then_inc(full(("vu", p)), 1)
                for p in range(T // 2):
                    wait(pe, "a_rot", b, 2 * (p // 2) + 2)
                    out = wait_free(pe, ("kt", p), b)
                    for i in range(2):
                        t = 2 * p + i
                        for g in range(G):
                            c = 2 * P * i + P * g
                            ins = PE.transpose(out[:, c:c + P], keyA[:, g, P * t:P * (t + 1)], ident[:])
                    ins.then_inc(full(("kt", p)), 1)
                for j in range(J):
                    out = wait_free(pe, ("KV", j), b)
                    for t in range(TB * j, TB * (j + 1)):
                        wait_drained(pe, ("kt", t // 2), b)
                        wait_drained(pe, ("vu", t // 2), b)
                        for g in range(G):
                            c = P * (t % TB) + 64 * g
                            ins = mm(out[:, c:c + 64], ktok[:, t, P * g:P * (g + 1)], vu[:, t, 64 * g:64 * g + 64], start=True, stop=True)
                    ins.then_inc(full(("KV", j)), 1)

                def energies(p):
                    wait(pe, "a_rot", b, 4 + 2 * (p // 2) + 2)
                    for r in range(4):
                        out = wait_free(pe, ("E", p, r), b)
                        for i in range(2):
                            for g in range(G):
                                c, t = 2 * P * i + P * g, 2 * p + i
                                ins = mm(out[:, c:c + P], keyA[32 * r:32 * r + 32, g, P * t:P * (t + 1)],
                                         qryA[32 * r:32 * r + 32, g, P * t:P * (t + 1)], start=True, stop=True)
                        ins.then_inc(full(("E", p, r)), 1)

                energies(0)
                wait(pe, "a_state", b, G)
                att = wait_free(pe, ("att",), b)
                for p in range(T // 2):
                    if p + 1 < T // 2:
                        energies(p + 1)
                    em = em0 if p % 2 else silu4
                    wait_drained(pe, ("E", p, 3), b)
                    for i in range(2):
                        t = 2 * p + i
                        out = att[:, t // TB, P * (t % TB):P * (t % TB + 1)]
                        for g in range(G):
                            mm(out[:, 64 * g:64 * g + 64], qryA[:, g, P * t:P * (t + 1)], st[:, t, 64 * g:64 * g + 64],
                               start=(t % TB == 0 and g == 0), stop=False, skip_group_check=True)
                        for h in range(H):
                            c = 2 * P * i + P * (h // 4)
                            ins = mm(out[:, HD * h:HD * (h + 1)], em[:, h % 4, c:c + P], vu[:, t, HD * h:HD * (h + 1)],
                                     start=False, stop=(t % TB == TB - 1 and h == H - 1), skip_group_check=True)
                ins.then_inc(full(("att",)), 1)
                wait_drained(pe, ("att",), b)
                for j in range(J):
                    out = wait_free(pe, ("yT", j), b)
                    for i in range(TB):
                        ins = PE.transpose(out[:, P * i:P * (i + 1)], y[:, TB * j + i, :], ident[:])
                    ins.then_inc(full(("yT", j)), 1)
                for j in range(J):
                    wait_drained(pe, ("yT", j), b)
                    out = wait_free(pe, ("ao", j), b)
                    mm(out[:, :], ow1[:], yT[:, BLK * j:BLK * (j + 1)], start=True, stop=True).then_inc(full(("ao", j)), 1)
                for j in range(J):
                    wait_drained(pe, ("ao", j), b)
                    layer_norm(b, j, z[:, j, :])

            def layer_norm(b, m, src):
                out = wait_free(pe, ("mean", m), b)
                mm(out[:, :], meanw[:], src, start=True, stop=True).then_inc(full(("mean", m)), 1)
                wait(pe, "ln_square", b, m + 1)
                out = wait_free(pe, ("var", m), b)
                mm(out[:, :], meanw[:], lnq[:, m % 2, :], start=True, stop=True).then_inc(full(("var", m)), 1)

            def scores(b, l, n):
                t, g = divmod(n, 2)
                if g == 0:
                    wait_drained(pe, ("kT", l, t), b)
                out = wait_free(pe, ("S", l, n), b)
                for e in range(2):
                    mm(out[:, e, 0:2 * KEYS], identb[:], ap3(band[:, min(t, 1), :], [[0, 2], [1, KEYS]]),
                       start=True, stop=False, skip_group_check=True)
                for e in range(2):
                    for r in range(2):
                        pr = 2 * g + r
                        ins = mm(out[:, e, KEYS * r:KEYS * (r + 1)], qTs[64 * e:64 * e + 64, t % 2, pr, :],
                                 keyT[64 * e:64 * e + 64, pr, P * t:P * t + KEYS], start=False, stop=(r == 1), skip_group_check=True)
                ins.then_inc(full(("S", l, n)), 1)

            def layer(b, l):
                for what, n in attention_steps():
                    if what == "proj" or what == "v":
                        wait(pe, "b_shift", b, 4 * l + 2 * (n // TB) + 2)
                        for name, c in ((("qp", 0), ("kp", INNER)) if what == "proj" else (("vp", 2 * INNER),)):
                            key = (name, l, n)
                            out = wait_free(pe, key, b)
                            mm(out[:, :], hT[:, P * n:P * (n + 1)], wqkv[:, l, c:c + INNER], start=True, stop=True).then_inc(full(key), 1)
                    elif what == "turn":
                        wait(pe, "b_qk", b, T * l + n + 1)
                        for w, name in enumerate(("qT", "kT")):
                            key = (name, l, n)
                            out = wait_free(pe, key, b)
                            for i in range(PAIRS):
                                ins = PE.transpose(out[:, P * i:P * (i + 1)], qk[:, n % 2, w, P * i:P * (i + 1)], ident[:])
                            ins.then_inc(full(key), 1)
                    elif what == "S":
                        scores(b, l, n)
                    elif what == "P":
                        wait_drained(pe, ("S", l, n), b)
                        out = wait_free(pe, ("Pc", l, n), b)
                        for i in range(4):
                            ins = PE.transpose(out[:, P * i:P * (i + 1)], prob[:, n % 2, i, P:2 * P], ident[:])
                        ins.then_inc(full(("Pc", l, n)), 1)
                        out = wait_free(pe, ("Pp", l, n), b)
                        apart(pe)
                        for i in range(4):
                            ins = PE.transpose(out[:, WIN * i:WIN * (i + 1)], prob[0:WIN, n % 2, i, 0:P], ident[0:WIN, 0:WIN])
                        ins.then_inc(full(("Pp", l, n)), 1)
                    elif what == "O":
                        t, g = divmod(n, 2)
                        wait_drained(pe, ("Pc", l, n), b)
                        wait_drained(pe, ("Pp", l, n), b)
                        apart(pe)
                        out = wait_free(pe, ("O", l, n), b)
                        for i in range(4):
                            h, c = 4 * g + 2 * (i % 2) + i // 2, slice((DH + 1) * i, (DH + 1) * (i + 1))
                            mm(out[:, c], PTc[:, n % 2, i, :], vring[:, t % 4, h, :], start=True, stop=False, skip_group_check=True)
                            ins = mm(out[0:WIN, c], PTp[:, n % 2, i, :], vring[:, (t - 1) % 4, h, :], start=False, stop=True, skip_group_check=True)
                        ins.then_inc(full(("O", l, n)), 1)
                    elif what == "oT":
                        wait_drained(pe, ("O", l, 2 * n + 1), b)
                        out = wait_free(pe, ("oT", l, n), b)
                        for i in range(4):
                            ins = PE.transpose(out[:, P * i:P * (i + 1)], oS[:, n % 2, P * i:P * (i + 1)], ident[:])
                        ins.then_inc(full(("oT", l, n)), 1)
                    else:
                        wait_drained(pe, ("oT", l, TB * n + TB - 1), b)
                        out = wait_free(pe, ("wo", l, n), b)
                        for i in range(4):
                            ins = mm(out[:, :], wo[:, l, i, :], oT[:, i, :], start=(i == 0), stop=(i == 3))
                        ins.then_inc(full(("wo", l, n)), 1)
                for j in range(J):
                    m = 2 + 2 * l + j
                    wait(pe, "f_shift", b, 4 * l + 2 * j + 2)
                    layer_norm(b, m, h2[:, :])
                    wait(pe, "f_hn", b, 2 * l + j + 1)
                    for f in range(FB):
                        w = FW[f]
                        for name, c in (("gate", HID + P * f), ("up", P * f)):
                            key = (name, l, j, f)
                            out = wait_free(pe, key, b)
                            mm(out[0:w, :], w1[:, l, c:c + w], hn[:, :], start=True, stop=True).then_inc(full(key), 1)
                    key = ("down", l, j)
                    wait_drained(pe, ("up", l, j, FB - 1), b)
                    out = wait_free(pe, key, b)
                    for f in range(FB):
                        w = FW[f]
                        ins = mm(out[:, :], w2[0:w, l, f, :], up[0:w, f, :], start=(f == 0), stop=(f == FB - 1))
                    ins.then_inc(full(key), 1)

            def sampling(b):
                for j in range(J):
                    wait(pe, "ln_out", b, 7 + j)
                    out = wait_free(pe, ("x2t", j), b)
                    for i in range(TB):
                        ins = PE.transpose(out[:, P * i:P * (i + 1)], x2[:, BLK * j + P * i:BLK * j + P * (i + 1)], ident[:])
                    ins.then_inc(full(("x2t", j)), 1)
                for t in range(T):
                    out = wait_free(pe, ("wk", t), b)
                    mm(out[:, 0:CW], x2[:, P * t:P * (t + 1)], wc[:], start=True, stop=True).then_inc(full(("wk", t)), 1)
                for t in range(T):
                    out = wait_free(pe, ("sum", t), b)
                    for c in range(NC_):
                        n = NC_ * t + c
                        wait(pe, "c_prod", b, n + 1)
                        for s in range(SC):
                            ins = mm(out[:, 0:2 * D], ident[:], gat[:, n % GB, s, :], start=(c == 0 and s == 0),
                                     stop=(c == NC_ - 1 and s == SC - 1))
                        ins.then_inc(SEM["c_read"] if c < NC_ - 1 else full(("sum", t)), 1)
                    if t % TB == TB - 1:
                        j = t // TB
                        wait_drained(pe, ("sum", t), b)
                        out = wait_free(pe, ("cT", j), b)
                        for i in range(TB):
                            ins = PE.transpose(out[:, P * i:P * (i + 1)], osum[:, TB * j + i, :], ident[:])
                        ins.then_inc(full(("cT", j)), 1)
                        wait_drained(pe, ("cT", j), b)
                        out = wait_free(pe, ("co", j), b)
                        for i in range(TB):
                            ins = mm(out[:, P * i:P * (i + 1)], cT[:, P * i:P * (i + 1)], ow2[:], start=True, stop=True)
                        ins.then_inc(full(("co", j)), 1)

            def experts(b):
                for j in range(J):
                    wait(pe, "c_x3", b, TB * (j + 1))
                    out = wait_free(pe, ("x3T", j), b)
                    for i in range(TB):
                        ins = PE.transpose(out[:, P * i:P * (i + 1)], x3[:, TB * j + i, :], ident[:])
                    ins.then_inc(full(("x3T", j)), 1)
                for j in range(J):
                    wait_drained(pe, ("x3T", j), b)
                    out = wait_free(pe, ("lg", j), b)
                    mm(out[0:E_, :], gw[:], x3T[:, BLK * j:BLK * (j + 1)], start=True, stop=True).then_inc(full(("lg", j)), 1)
                wait(pe, "d_max", b, 3)
                out = wait_free(pe, ("pT",), b)
                apart(pe)
                for t in range(T):
                    ins = PE.transpose(out[:, E_ * t:E_ * (t + 1)], lgS[:, P * t:P * (t + 1)], ident[0:E_, 0:E_])
                ins.then_inc(full(("pT",)), 1)
                wait(pe, "d_rank", b, 7)
                for j in range(J):
                    out = wait_free(pe, ("iT", j), b)
                    for i in range(TB):
                        t = TB * j + i
                        ins = PE.transpose(out[0:E_, P * i:P * (i + 1)], ind[:, E_ * t:E_ * (t + 1)], ident[:])
                    ins.then_inc(full(("iT", j)), 1)
                for what, q in moe_steps():
                    e, j = divmod(q, 2)
                    out = wait_free(pe, (what, q), b)
                    if what == "h1":
                        ins = mm(out[:, :], m1[:, e, :], x3T[:, BLK * j:BLK * (j + 1)], start=True, stop=True)
                    elif what == "h2":
                        wait_drained(pe, ("h1", q), b)
                        ins = mm(out[:, :], m2[:, e, :], h1s[:, q % 2, :], start=True, stop=True)
                    elif what == "y":
                        wait_drained(pe, ("h2", q), b)
                        for i in range(TB):
                            ins = mm(out[:, P * i:P * (i + 1)], h2s[:, q % 2, P * i:P * (i + 1)], m3[:, e, :], start=True, stop=True)
                    else:
                        wait(pe, "d_relu", b, q + 1)
                        for i in range(TB):
                            ins = mm(out[:, 0:1], ys[:, q % 4, P * i:P * (i + 1)], wt[:, TB * j + i, e:e + 1], start=(i == 0), stop=(i == TB - 1))
                    ins.then_inc(full((what, q)), 1)

            def batch(b):
                first_attention(b)
                for l in range(LAYERS):
                    layer(b, l)
                for j in range(J):
                    wait(pe, "f_res", b, j + 1)
                    layer_norm(b, 6 + j, z[:, j, :])
                sampling(b)
                experts(b)

            batch(0)
            with pe.Fori(1, B) as b:
                batch(b)
            for c in CB:
                pe.wait_ge(drained[c], B * turns[c])
            pe.wait_ge(SEM["a_rot"], 8 * B)
            PE.transpose(psum["c0"][0:E_, 0:D], vacc[:], ident[:]).then_inc(last["filled"], 1)
            pe.wait_ge(last["vt"], 1)
            pe.wait_ge(last["ind"], 16)
            for i in range(B * J):
                if i >= 2:
                    pe.wait_ge(last["z"], i - 1)
                for t in range(TB):
                    c = BLK * i + P * t
                    ins = mm(psum[CB[i % 2]][:, P * t:P * (t + 1)], indT[:, c:c + P], v8[:], start=True, stop=True)
                ins.then_inc(last["filled"], 1)


def kernel(**inputs):
    import numpy as np
    import concourse.bacc as _bacc
    from concourse.bass_utils import run_bass_kernel_spmd as _run

    f = lambda n: np.ascontiguousarray(np.asarray(inputs[n]))
    c = np.ascontiguousarray

    rows = np.array([(4 * g + r) * HD + d for g in range(G) for r in range(4) for _ in range(2) for d in range(HD)])
    w, wb = f("L0_attn_qkvu_w"), f("L0_attn_qkvu_b")
    host = {"x": f("L0_attn_x")}
    host["wkq"] = c(np.stack([w[D + rows].T, w[rows].T], 1))
    host["wvu"] = c(w[2 * D:].T)
    host["kqb"] = c(np.stack([wb[D + rows].reshape(G, P).T, wb[rows].reshape(G, P).T], 1))
    host["vub"] = c(wb[2 * D:])
    host["ow1"] = c(f("L0_attn_out_w").T)
    host["wqkv"] = c(f("L0_ffn_wqkv").transpose(1, 0, 2))
    host["wo"] = c(f("L0_ffn_wo").reshape(LAYERS, 4, P, D).transpose(2, 0, 1, 3))
    host["w1"] = c(f("L0_ffn_w1").transpose(1, 0, 2))

    def pad(a, n, axis):
        width = [(0, 0)] * a.ndim
        width[axis] = (0, n - a.shape[axis])
        return np.pad(a, width)

    host["w2"] = c(pad(f("L0_ffn_w2"), FB * P, 1).reshape(LAYERS, FB, P, D).transpose(2, 0, 1, 3))
    kw, kb = f("L1_attn_kernel_w").reshape(H, KS, D)[:, :S], f("L1_attn_kernel_b").reshape(H, KS)[:, :S]
    host["wc"] = c(np.concatenate([f("L1_attn_wave_w"), kw.reshape(H * S, D)]).T)
    host["cb"] = c(np.concatenate([f("L1_attn_wave_b"), kb.reshape(-1)]))
    host["ow2"] = c(f("L1_attn_out_w").T)
    host["gw"] = f("L1_ffn_gate_w")
    host["gb"] = f("L1_ffn_gate_b").reshape(E_, 1)
    for i in (1, 2, 3):
        host[f"m{i}"] = c(f(f"L1_ffn_w{i}").transpose(1, 0, 2))
    host["b3"] = f("L1_ffn_b3").reshape(-1)
    slope = f("L0_attn_slope_rate").reshape(H)
    host["slope"] = slope
    host["slope_c"] = c(slope[rows // HD].reshape(G, P).T)
    theta = f("L0_attn_theta").reshape(-1)[rows].reshape(G, P).T
    b1 = pad(f("L0_ffn_b1").reshape(LAYERS, 2, HID), FB * P, 2).reshape(LAYERS, 2, FB, P)
    phase = np.tile(np.repeat(np.array([np.pi / 2, 0.0], np.float32), HD), 4).reshape(P, 1)
    ones = np.ones((P, 1), np.float32)
    columns = [f("L0_attn_out_b").reshape(P, 1), f("L0_ffn_ln_g").T, f("L0_ffn_ln_b").T,
               b1[:, 1].reshape(-1, P).T, b1[:, 0].reshape(-1, P).T, f("L0_ffn_b2").T,
               f("L1_ffn_b1").T, f("L1_ffn_b2").T, theta, phase, ones * np.float32(LN_EPS)]
    columns = np.concatenate(columns, 1)
    host["cols"] = c(pad(columns, 64, 1))
    qs, ks = f("L0_ffn_q_scale"), f("L0_ffn_k_scale")
    turn = (np.arange(DH) + DH // 2) % DH
    host["qkscale"] = c(np.stack([np.stack([qs, ks], 1), np.stack([qs[:, turn], ks[:, turn]], 1)], 1).reshape(LAYERS * 256))

    f4 = np.float32
    half_idx = np.arange(0, DH, 2, dtype=f4)
    inv_freq = (f4(1.0) / np.power(f4(10000.0), half_idx / f4(DH))).astype(f4)
    tt = np.arange(N, dtype=f4)
    freqs = (tt[:, None] * inv_freq[None, :]).astype(f4)
    freqs = np.concatenate([freqs, freqs], -1).astype(np.float64)
    bs = ((half_idx + f4(0.4 * DH)) / f4(1.4 * DH)).astype(np.float64)
    power = (tt.astype(np.float64) - N // 2) / float(WIN // 2)
    sc = bs[None, :] ** power[:, None]
    sc = np.concatenate([sc, sc], -1)
    sign = np.where(np.arange(DH) < DH // 2, -1.0, 1.0)[None]
    cs, sn = np.cos(freqs), np.sin(freqs) * sign
    tab = np.stack([cs * sc * 8.0, cs / sc, sn * sc * 8.0, sn / sc], 1).astype(f4)
    host["rbase"] = c(tab.reshape(T, P, 256).transpose(1, 0, 2))
    i, k = np.arange(P)[:, None], np.arange(KEYS)[None] - WIN
    seen = (k <= i) & (i <= k + WIN)
    bf = mybir.dt.to_np(BF16) if hasattr(mybir.dt, "to_np") else None
    import ml_dtypes
    bf = ml_dtypes.bfloat16
    host["band"] = c(np.stack([np.where(seen & (k >= 0), 0.0, MASKED), np.where(seen, 0.0, MASKED)], 1).astype(bf))
    host["ident"] = np.eye(P, dtype=f4)
    host["tri"] = (np.arange(P)[:, None] <= np.arange(P)[None]).astype(f4)
    host["blockd"] = (np.arange(P)[:, None] // 32 == np.arange(64)[None] // HD).astype(f4)
    host["posr"] = np.arange(N, dtype=f4)
    host["sidx"] = np.arange(S, dtype=f4) - 16
    host["base"] = c((np.arange(T)[None] * P + np.arange(P)[:, None]).astype(f4))
    host["ties"] = (np.arange(E_)[None] < np.arange(E_)[:, None]).astype(f4).reshape(-1)

    nc = _bacc.Bacc("TRN2", target_bir_lowering=False, num_devices=1)
    arrays, dram = {}, {}
    for name, a in host.items():
        arrays[f"in_{name}"] = a
        dram[name] = nc.dram_tensor(f"in_{name}", a.shape, mybir.dt.from_np(a.dtype), kind="ExternalInput").ap()
    out = nc.dram_tensor("out", (B, N, D), F32, kind="ExternalOutput").ap()

    def everywhere(row, n):
        return bass.AP(tensor=row.tensor, offset=row.offset, ap=[[0, P], [1, n]])

    def loads(v):
        full = lambda n: (v[n][:], dram[n])
        out_ = [full(n) for n in ("ident", "cols", "kqb", "wkq", "wvu", "slope_c", "blockd", "ow1", "wqkv", "wo", "w1", "w2", "wc", "ow2",
                                  "gw", "gb", "m1", "m2", "m3", "band", "base")]
        out_ += [(v["rbase"], dram["rbase"]), (v["tri"], dram["tri"])]
        for n in ("vub", "cb", "b3", "slope", "sidx"):
            out_.append((v[n][:], everywhere(dram[n], dram[n].shape[0])))
        out_.append((v["posr"], everywhere(dram["posr"], N)))
        out_.append((v["qkscale"].rearrange("p l c -> p (l c)"), everywhere(dram["qkscale"], LAYERS * 256)))
        out_.append((v["ties"][:].rearrange("p a b -> p (a b)"), everywhere(dram["ties"], E_ * E_)))
        return out_

    rows_of = lambda t, b: t[b * N:(b + 1) * N] if isinstance(b, int) else t[bass.ds(b * N, N)]
    A = {"x": dram["x"], "loads": loads,
         "x3v": lambda t, b: rows_of(t, b).rearrange("(t p) d -> p t d", p=P),
         "outv": lambda i: out[i // J, BLK * (i % J):BLK * (i % J + 1)].rearrange("(t p) d -> p t d", p=P)}
    build(nc, A)
    r = _run(nc, [arrays], core_ids=[0])
    return r.results[0]["out"]
```

```python
from contextlib import ExitStack

import concourse.bass as bass
from concourse import mybir

F32 = mybir.dt.float32
BF16 = mybir.dt.bfloat16
I32 = mybir.dt.int32
U32 = mybir.dt.uint32
ALU = mybir.AluOpType
ACT = mybir.ActivationFunctionType
AXX = mybir.AxisListType.X

P = 128
B, N, D = 4, 1024, 128
T = N // P
BLK = 512
J = N // BLK
TB = BLK // P
LN_EPS = 1e-5

H, HD = 8, 16
G = 2
RMS_EPS = 1e-6
TWO_PI_HI, TWO_PI_MID, TWO_PI_LO = 6.28125, 0.0019350051879882812, 3.0199159819e-07
PI_IN = 3.1415925
ROUND = 12582912.0

LAYERS, HB, DH, WIN = 2, 8, 64, 64
INNER = HB * DH
PAIRS = HB // 2
HID = int(D * 4 * 2 / 3)
FB = -(-HID // P)
FW = [min(P, HID - P * i) for i in range(FB)]
KEYS = WIN + P
MASKED = -1e30
UNITS = 2 * T

S, KS = 33, 64
CW = 2 * H + H * S
SC = 3
NCH = S // SC
CHUNKS = T * NCH
BCH = TB * NCH
SHARE = 4
GB = 5
LAG = 2

E_ = 8


def ap3(tensor_ap, dims):
    return bass.AP(tensor=tensor_ap.tensor, offset=tensor_ap.offset, ap=[tensor_ap.ap[0]] + [list(d) for d in dims])


def plan(keys):
    where, turns, nxt = {}, {}, {}
    for key, pool in keys:
        i = nxt.get(pool, 0)
        bank = pool[i % len(pool)]
        nxt[pool] = i + 1
        where[key] = (bank, turns.get(bank, 0))
        turns[bank] = turns.get(bank, 0) + 1
    return where, turns


PROJ, SCORE, TURN, CB = ("pa", "pb"), ("sc",), ("ta", "tb"), ("c0", "c1")


TILE = [("S", 0), ("P", -1), ("proj", 2), ("turn", 1), ("X", 0), ("O", -1), ("rn", 2), ("S", 1),
        ("P", 0), ("X", 1), ("rot", 2), ("v", 1), ("oT", -1), ("wo", -1), ("O", 0)]


def attention_steps(l):
    steps = [(what, l, 0) for what in ("proj", "rn", "rot", "turn", "v")] + [(what, l, 1) for what in ("proj", "rn", "rot")]
    for t in range(T + 1):
        for what, ahead in TILE:
            if what in "SXPO":
                if 0 <= 2 * t + ahead < UNITS:
                    steps.append((what, l, 2 * t + ahead))
            elif what == "wo":
                if t and t % TB == 0:
                    steps.append((what, l, t // TB - 1))
            elif (0 if what == "oT" else ahead) <= t + ahead < T:
                steps.append((what, l, t + ahead))
    return steps


def norm_steps(m):
    return [("mean", m), ("var", m)]


def feed_forward_steps(l, j):
    return norm_steps(2 + 2 * l + j) + [("ff", l, j, f) for f in range(FB)] + [("down", l, j)]


def spread(main, side):
    out, done, held = [], 0, False
    for i, step in enumerate(main):
        out.append(step)
        held = step[0] == "proj" or held and step[0] != "rn"
        while not held and done < len(side) and (done + 1) * len(main) <= (i + 1) * len(side):
            out.append(side[done])
            done += 1
    return out + side[done:]


def first_steps():
    steps = [("xT",)] + [("kq", i) for i in range(2 * J * G)] + [("vu",), ("kt",), ("KV",), ("E", 0)]
    for p in range(T // 2):
        if p + 1 < T // 2:
            steps.append(("E", p + 1))
        steps.append(("heads", p))
    steps += [("y",), ("ao",), ("mean", 0), ("mean", 1), ("var", 0), ("var", 1), ("shift", 0, 0), ("shift", 0, 1)]
    a0, a1 = attention_steps(0), attention_steps(1)
    i0, i1 = a0.index(("wo", 0, 0)) + 1, a1.index(("wo", 1, 0)) + 1
    k1 = a1.index(("proj", 1, TB))
    steps += a0[:i0] + spread(a0[i0:], feed_forward_steps(0, 0)) + [("shift", 1, 0)]
    steps += spread(a1[:k1], feed_forward_steps(0, 1) + [("shift", 1, 1)]) + a1[k1:i1]
    steps += spread(a1[i1:], feed_forward_steps(1, 0))
    return steps + spread(feed_forward_steps(1, 1), norm_steps(6)) + norm_steps(7)


def moe_steps():
    out = []
    for q in range(2 * E_ + 3):
        for what, lag in (("h1", 0), ("h2", 1), ("y", 2), ("vs", 3)):
            if 0 <= q - lag < 2 * E_:
                out.append((what, q - lag))
    return out


def second_steps():
    steps = [("x2t", j) for j in range(J)] + [("wk", t) for t in range(T)] + [("pos",), ("w", 0)]
    for n in range(CHUNKS + LAG):
        if n < CHUNKS:
            steps.append(("g", n))
            if n % NCH == NCH // 2 and n // NCH + 1 < T:
                steps.append(("w", n // NCH + 1))
        if n >= LAG:
            steps.append(("acc", n - LAG))
            if (n - LAG + 1) % BCH == 0:
                j = (n - LAG) // BCH
                steps += [("cT", j), ("co", j)]
    steps += [("x3T", j) for j in range(J)] + [("lg", j) for j in range(J)] + [("soft",), ("rank",), ("iT",)]
    return steps + moe_steps()


FIRST, SECOND = first_steps(), second_steps()
ROOM = {"xT": 2, "kq": 0.5, "vu": 0.5, "kt": 3, "KV": 4, "E": 5, "heads": 3, "y": 3, "ao": 2, "mean": 2, "var": 0, "shift": 1, "proj": 0,
        "rn": 2, "rot": 0.75, "turn": 1.5, "v": 0, "S": 0, "P": 0, "X": 2, "O": 1, "oT": 1, "wo": 1, "ff": 1, "down": 2}
NEED = {"g": 1, "cT": 1, "co": 3, "x3T": 2, "lg": 2, "soft": 5,
        "rank": 3.2, "iT": 3, "h1": 0.35, "h2": 0.32, "y": 0.35, "vs": 0.35}
HEAD = 2 + T + 2
FIRST_KEYS = {
    "xT": lambda: [(("xT", j), PROJ) for j in range(J)],
    "kq": lambda i: [(("kq", i), PROJ)],
    "vu": lambda: [(("vu", p), PROJ) for p in range(T // 2)],
    "kt": lambda: [(("kt", p), TURN) for p in range(T // 2)],
    "KV": lambda: [(("KV", j), TURN) for j in range(J)],
    "E": lambda p: [(("E", p, r), (("pa", "pb", "ta", "tb")[r],)) for r in range(4)],
    "heads": lambda p: [(("att",), SCORE)] if p == 0 else [],
    "y": lambda: [(("yT", j), PROJ) for j in range(J)],
    "ao": lambda: [(("ao", j), PROJ) for j in range(J)],
    "mean": lambda m: [(("mean", m), PROJ)],
    "var": lambda m: [(("var", m), PROJ)],
    "shift": lambda l, j: [], "rn": lambda l, t: [], "rot": lambda l, t: [], "X": lambda l, n: [],
    "proj": lambda l, t: [(("qp", l, t), PROJ), (("kp", l, t), PROJ)],
    "v": lambda l, t: [(("vp", l, t), PROJ)],
    "turn": lambda l, t: [(("qT", l, t), TURN), (("kT", l, t), TURN)],
    "S": lambda l, n: [(("S", l, n), SCORE)],
    "P": lambda l, n: [(("Pc", l, n), TURN), (("Pp", l, n), TURN)],
    "O": lambda l, n: [(("O", l, n), TURN)],
    "oT": lambda l, t: [(("oT", l, t), TURN)],
    "wo": lambda l, j: [(("wo", l, j), PROJ)],
    "ff": lambda l, j, f: [(("gate", l, j, f), PROJ), (("up", l, j, f), PROJ)],
    "down": lambda l, j: [(("down", l, j), PROJ)],
}
SECOND_KEYS = {
    "pos": lambda: [], "w": lambda t: [], "g": lambda n: [], "cT": lambda j: [], "rank": lambda: [],
    "acc": lambda n: [(("sum", n // BCH), ("c0",))] if n % BCH == 0 else [],
    "co": lambda j: [(("co", j), ("c1",))],
    "soft": lambda: [(("pT",), CB)],
    "iT": lambda: [(("iT", j), CB) for j in range(J)],
    **{k: (lambda k: lambda i: [((k, i), CB)])(k) for k in ("x2t", "wk", "x3T", "lg", "h1", "h2", "y", "vs")},
}


def first_keys():
    return [k for what, *n in FIRST for k in FIRST_KEYS[what](*n)]


def second_keys():
    return [k for what, *n in SECOND for k in SECOND_KEYS[what](*n)]


def both_steps():
    first, second = [("first", *x) for x in FIRST], [("second", *x) for x in SECOND]
    room = sum(ROOM[what] for what, *_ in FIRST)
    need = sum(NEED.get(what, 0) for what, *_ in SECOND[HEAD:])
    out, given, taken, done = second[:HEAD], 0, 0, HEAD
    for step in first:
        out.append(step)
        given += ROOM[step[1]] / room
        while done < len(second) and taken + NEED.get(second[done][1], 0) / need <= given + 1e-9:
            taken += NEED.get(second[done][1], 0) / need
            out.append(second[done])
            done += 1
    return out + second[done:]


def build(nc, A):
    ab_where, ab_turns = plan(first_keys())
    cd_where, cd_turns = plan(second_keys())
    where = {**ab_where, **cd_where}
    turns = {**ab_turns, **cd_turns}

    with ExitStack() as ctx:
        def sb(name, shape, dt=F32):
            return ctx.enter_context(nc.sbuf_tensor(name, shape, dt))

        psum = {n: ctx.enter_context(nc.psum_tensor(n, [P, BLK], F32)) for n in ("pa", "pb", "ta", "tb", "c0", "c1")}
        psum["sc"] = ctx.enter_context(nc.psum_tensor("sc", [P, 2, BLK], F32))

        wkq = sb("wkq", [P, 2, G * P])
        wvu = sb("wvu", [P, 2 * D])
        ow1 = sb("ow1", [P, D])
        wqkv = sb("wqkv", [P, LAYERS, 3 * INNER])
        wo = sb("wo", [P, LAYERS, 4, D])
        w1 = sb("w1", [P, LAYERS, 2 * HID])
        w2 = sb("w2", [P, LAYERS, FB, D])
        wc = sb("wc", [P, CW])
        ow2 = sb("ow2", [P, D])
        gw = sb("gw", [P, E_])
        mw = sb("mw", [P, 2, 4, D])
        kqb = sb("kqb", [P, 2, G])
        vub = sb("vub", [P, 2 * D])
        cols = sb("cols", [P, 64])
        ident = sb("ident", [P, P])
        identb = sb("identb", [P, P], BF16)
        meanw = sb("meanw", [P, P])
        blockd = sb("blockd", [P, D // G])
        band = sb("band", [P, 2, KEYS], BF16)
        emask = sb("emask", [P, 4, G, P])
        es = sb("es", [P, G])
        csT = sb("csT", [P, G, N])
        rot = sb("rot", [P, LAYERS, T, 2, 2, DH])
        cb = sb("cb", [P, CW])
        sidx = sb("sidx", [P, S])
        base = sb("base", [P, T])
        ties = sb("ties", [P, E_, E_])
        gb = sb("gb", [E_, 1])
        slope = sb("slope", [P, H])
        slope_c = sb("slope_c", [P, G])
        OB, LG, LB, BG, BA, B2, C1, C2, TH, PH, EPS, REPS, LN256 = 0, 1, 3, 5, 11, 17, 19, 27, 35, 37, 38, 39, 40

        def col(i, rows=P):
            return cols[0:rows, i:i + 1]

        x1 = sb("x1", [P, 1 + N])
        xb = sb("xb", [P, 1 + N])
        xm = sb("xm", [P, 1 + N])
        x2 = xm[:, 1:1 + N]
        x2tok = sb("x2tok", [P, T, D])
        lnc = sb("lnc", [P, 2, BLK])
        lnq = sb("lnq", [P, 2, BLK])
        keyT = sb("keyT", [P, 3, PAIRS, P])
        vring = sb("vring", [P, 3, HB, DH + 1])
        prob = sb("prob", [P, 2, 4, 2 * P])
        SIZE_A, SIZE_C = 11264, 9632
        pool_a = sb("pool_a", [P, SIZE_A])
        pool_c = sb("pool_c", [P, SIZE_C])
        used = {"a": 0, "b": 0, "c": 0}

        def part(which, *shape):
            n = 1
            for s in shape:
                n *= s
            at = used[which]
            used[which] = at + n
            v = (pool_c if which == "c" else pool_a)[:, at:at + n]
            if len(shape) == 1:
                return v
            names = " ".join(f"d{i}" for i in range(len(shape)))
            return v.rearrange(f"p ({names}) -> p {names}", **{f"d{i}": s for i, s in enumerate(shape)})

        keyA = part("a", G, N)
        qryA = part("a", G, N)
        silu4 = part("a", 4, BLK)
        ktok = silu4.rearrange("p a (b c) -> p (a b) c", b=2)
        pre = part("a", T, D)
        st = pre
        KV = part("a", T, D)
        suf = part("a", T, D)
        em0 = pool_a[:, used["a"] - 2 * T * D:used["a"]].rearrange("p (a b) -> p a b", a=4)
        vu = part("a", T, 2 * D)
        y = KV
        yT = suf.rearrange("p a b -> p (a b)")
        xtok = sb("xtok", [P, T, D])
        ss1 = sb("ss1", [P, 3, T])
        hT = part("b", N)
        sq = part("b", 2, BLK)
        qn = part("b", 2, HB, DH)
        r2 = part("b", 2, HB, DH)
        qk = part("b", 2, INNER)
        qTs = part("b", 2, PAIRS, P)
        PTc = part("b", 2, 4, P)
        PTp = part("b", 2, 4, WIN)
        oS = part("b", 2, INNER)
        oT = part("b", 4, BLK)
        h2 = part("b", BLK)
        hn = h2
        up = sb("up", [P, FB, BLK])
        ssq = sb("ssq", [P, 2, 2, 16])
        newt = sb("newt", [P, 16])
        nmax = sb("nmax", [P, 2, 4])
        rsum = sb("rsum", [P, 2, 4])
        wk = part("c", T, CW)
        sgt = part("c", 2, T, H)
        fp = part("c", 4, T)
        pos = part("c", T, S)
        lo = part("c", T, S)
        tmp = pos
        frac = part("c", T * S, 2)
        idx = sb("idx", [P, T, S], U32)
        wlh = part("c", 2, S, 2, H)
        gat = part("c", GB, SC, 2 * D)
        psums = part("c", 2, D)
        zc = part("c", TB, D)
        cT = part("c", BLK)
        bn = sb("bn", [P, T, 6])
        mv = sb("mv", [P, T, 2])
        rst = sb("rst", [P, 2, T])
        x3 = x2tok
        cf = pool_c[:, :]
        x3T = cf[:, 0:N]
        lgS = cf[0:E_, N:2 * N]
        rk1 = cf[:, 2 * N:2 * N + 512].rearrange("p (t e f) -> p t e f", t=T, e=E_)
        rk2 = cf[:, 2 * N + 512:3 * N].rearrange("p (t e f) -> p t e f", t=T, e=E_)
        h1s = cf[:, 3 * N:4 * N].rearrange("p (a b) -> p a b", a=2)
        h2s = cf[:, 4 * N:5 * N].rearrange("p (a b) -> p a b", a=2)
        ys = cf[:, 5 * N:7 * N].rearrange("p (a b) -> p a b", a=4)
        lgs = sb("lgs", [E_, 3])
        prT = sb("prT", [P, T, E_])
        cnt = sb("cnt", [P, T * E_])
        ind = sb("ind", [P, T * E_])
        wt = sb("wt", [P, T, E_])
        indT = pool_a[0:E_, 0:B * N]
        fin = pool_a[:, B * N:B * N + 2 * BLK].rearrange("p (t d) -> p t d", d=D)
        vacc = sb("vacc", [P, E_])
        v8 = sb("v8", [E_, D])
        assert max(used["a"], used["b"]) <= SIZE_A and used["c"] <= SIZE_C, used
        posr = pool_a[:, 0:N]
        ang = pool_a[:, N:3 * N].rearrange("p (g n) -> p g n", g=G)
        kk = pool_a[:, 3 * N:5 * N].rearrange("p (g n) -> p g n", g=G)
        rbase = pool_a[:, 5 * N:7 * N].rearrange("p (t c) -> p t c", t=T)
        qkscale = pool_a[:, 7 * N:7 * N + 512].rearrange("p (l c) -> p l c", l=LAYERS)
        tri = pool_a[:, 8 * N:8 * N + P]

        table = nc.dram_tensor("rows_of_x2", (N + 1, 2 * D), F32, kind="Internal").ap()
        ind_dram = nc.dram_tensor("chosen_experts", (B, E_, N), F32, kind="Internal").ap()
        x3_dram = nc.dram_tensor("x3_of_all", (B * N, D), F32, kind="Internal").ap()

        PER = {
            "x_loaded": 16, "a_rot": 8, "a_scan": 16, "a_state": 2, "a_square": 8, "a_rstd": 2,
            "ln_square": 8, "ln_rstd": 8, "ln_out": 8,
            "b_shift": 8, "b_square": 32, "b_ss": 32, "b_rn": 32, "b_cos": 16, "b_sin": 32, "b_qk": 16,
            "b_max": 32, "b_recip": 32, "b_newton": 48, "a_newton": 4, "c_newton": 8, "f_shift": 8, "f_hn": 4, "f_res": 2,
            "c_silu": 1, "c_act": 2, "c_pos": 13, "c_w": T, "c_table": 64, "c_prod": CHUNKS + CHUNKS // SHARE, "c_acc": CHUNKS - J,
            **{f"c_gather{i}": 16 * SC * -(-(CHUNKS - i) // GB) for i in range(GB)},
            "c_z": 2, "c_bn": 16, "c_rstd": 4, "c_x3": 8, "c_saved": 16,
            "d_max": 3, "d_exp": 1, "d_rank": 7, "d_relu": 2 * E_, "d_expert0": 16 * E_, "d_expert1": 16 * E_, "d_saved": 16,
        }
        AHEAD = {n for n in PER if n[:2] in ("c_", "d_") and not n.startswith("c_gather")}
        SEM = {n: ctx.enter_context(nc.semaphore(n)) for n in PER}
        filled = {n: ctx.enter_context(nc.semaphore(f"{n}_filled")) for n in psum}
        drained = {n: ctx.enter_context(nc.semaphore(f"{n}_drained")) for n in psum}
        loaded = ctx.enter_context(nc.semaphore("weights_loaded"))
        setup = {n: ctx.enter_context(nc.semaphore(f"setup_{n}")) for n in ("dve", "act", "pool", "ready")}
        last = {n: ctx.enter_context(nc.semaphore(f"final_{n}")) for n in ("filled", "drained", "vt", "x0", "x1", "bn", "rstd", "newton", "out", "stored0", "stored1", "z", "ind")}

        def reach(eng, sem, value):
            if not isinstance(value, int) or value > 0:
                eng.wait_ge(sem, value)
                if not isinstance(value, int) and eng in (nc.gpsimd, nc.sync):
                    apart(eng)

        def apart(eng):
            eng.nop(nofuse=True)

        def wait(eng, name, b, n):
            reach(eng, SEM[name], (b + (name in AHEAD)) * PER[name] + n)

        def wait_filled(eng, key, b):
            bank, n = where[key]
            reach(eng, filled[bank], (b + (bank in CB)) * turns[bank] + n + 1)
            return psum[bank]

        def wait_drained(eng, key, b):
            bank, n = where[key]
            reach(eng, drained[bank], (b + (bank in CB)) * turns[bank] + n + 1)

        def wait_free(eng, key, b):
            bank, n = where[key]
            reach(eng, drained[bank], (b + (bank in CB)) * turns[bank] + n)
            return psum[bank]

        def full(key):
            return filled[where[key][0]]

        def empty(key):
            return drained[where[key][0]]

        def run(eng, first, second):
            for s in FIRST:
                first(0, *s)
            with eng.Fori(1, B) as b:
                for part_, *s in both_steps():
                    if part_ == "first":
                        first(b, *s)
                    else:
                        second(b - 1, *s)
            for s in SECOND:
                second(B - 1, *s)

        def on_vector(n):
            return n % SHARE == SHARE - 1

        def products(n):
            return n + 1 + (n + 1) // SHARE

        def chunk_added(eng, b, n):
            if n % BCH == BCH - 1:
                wait_filled(eng, ("sum", n // BCH), b)
            else:
                wait(eng, "c_acc", b, n + 1 - n // BCH)

        def gel(l, j, f):
            return (lnc, lnq)[f % 2][:, (2 + 2 * l + j) % 2, :]

        weight_loads = A["loads"](locals())
        n_loads = len(weight_loads)

        block = ctx.enter_context(nc.Block())

        @block.sync
        def _(sp):
            sp.wait_ge(setup["ready"], 1)

            def first(b, what, *a):
                if what == "xT":
                    wait_drained(sp, ("xT", J - 1), b - 1)
                    sp.dma_start(xtok[:], A["batch"](A["x"], b)).then_inc(SEM["x_loaded"], 16)

            def load_expert(b, e):
                if e < 2:
                    wait_drained(sp, ("y", 2 * E_ - 1), b - 1)
                else:
                    wait_drained(sp, ("y", 2 * (e - 2) + 1), b)
                sp.dma_start(mw[:, e % 2, 0:3, :], A["experts"][e]).then_inc(SEM[f"d_expert{e % 2}"], 16)
                sp.dma_start(mw[:, e % 2, 3, :], A["everywhere"](A["b3"], D * e, D)).then_inc(SEM[f"d_expert{e % 2}"], 16)

            def second(b, what, *a):
                if what == "x2t" and a[0] == J - 1:
                    wait_drained(sp, ("x2t", J - 1), b)
                    wait(sp, "c_prod", b, 0)
                    rows = table[:, D:2 * D]
                    sp.dma_start(table[1:N + 1, 0:D].rearrange("(t p) d -> p t d", p=P), x2tok[:]).then_inc(SEM["c_table"], 16)
                    sp.dma_start(rows[0:N].rearrange("(t p) d -> p t d", p=P), x2tok[:]).then_inc(SEM["c_table"], 16)
                    sp.dma_start(table[0:1, 0:D], x2tok[0:1, 0, :]).then_inc(SEM["c_table"], 16)
                    sp.dma_start(rows[N:N + 1], x2tok[P - 1:P, T - 1, :]).then_inc(SEM["c_table"], 16)
                elif what == "co" and a[0] == J - 1:
                    wait(sp, "c_x3", b, T)
                    sp.dma_start(A["batch"](A["flat"](x3_dram), b), x3[:]).then_inc(SEM["c_saved"], 16)
                    for e in range(2):
                        load_expert(b, e)
                elif what == "iT":
                    wait_drained(sp, ("iT", J - 1), b)
                    sp.dma_start(ind_dram[b] if isinstance(b, int) else ind_dram[bass.ds(b, 1)].rearrange("b e n -> (b e) n"), lgS).then_inc(SEM["d_saved"], 16)
                elif what == "y" and a[0] % 2 and a[0] // 2 + 2 < E_:
                    load_expert(b, a[0] // 2 + 2)

            for dst, src in weight_loads:
                sp.dma_start(dst, src).then_inc(loaded, 16)
            run(sp, first, second)
            sp.wait_ge(SEM["c_saved"], 16 * (B + 1))
            sp.wait_ge(SEM["d_saved"], 16 * (B + 1))
            sp.dma_start(indT.rearrange("e (b n) -> e b n", b=B), ind_dram.rearrange("b e n -> e b n")).then_inc(last["ind"], 16)
            sp.wait_ge(last["filled"], 1)
            for i in range(B * J):
                if i >= 2:
                    sp.wait_ge(last["z"], i - 1)
                sp.dma_start(x2tok[:, TB * (i % 2):TB * (i % 2) + TB, :],
                             x3_dram[BLK * i:BLK * i + BLK].rearrange("(t p) d -> p t d", p=P)).then_inc(last[f"x{i % 2}"], 16)
                if i >= 1:
                    sp.wait_ge(last["out"], TB * i)
                    sp.dma_start(A["outv"](i - 1), fin[:, TB * ((i - 1) % 2):TB * ((i - 1) % 2) + TB, :]).then_inc(last[f"stored{(i - 1) % 2}"], 16)
            sp.wait_ge(last["out"], TB * B * J)
            sp.dma_start(A["outv"](B * J - 1), fin[:, TB:2 * TB, :]).then_inc(last["stored1"], 16)
            sp.wait_ge(last["stored0"], 8 * B * J)
            sp.wait_ge(last["stored1"], 8 * B * J)

        @block.gpsimd
        def _(pool):
            for name in sorted(AHEAD):
                pool.sem_inc(SEM[name], PER[name])
            for bank in CB:
                pool.sem_inc(filled[bank], turns[bank])
                pool.sem_inc(drained[bank], turns[bank])
            pool.sem_inc(setup["ready"], 1)
            nc.gpsimd.memset(x1[:, 0:1], 0.0)
            nc.gpsimd.memset(xb[:, 0:1], 0.0)
            nc.gpsimd.memset(xm[:, 0:1], 0.0)
            nc.gpsimd.memset(keyT[:], 0.0)
            nc.gpsimd.memset(prob[:], 0.0)
            nc.gpsimd.memset(vring[:], 1.0)
            nc.gpsimd.memset(vacc[:], 0.0)
            nc.gpsimd.memset(meanw[:], 1.0 / D).then_inc(setup["pool"], 1)
            pool.wait_ge(setup["pool"], 1)

            def first(b, what, *a):
                pass

            def gather(b, n):
                if n >= GB:
                    chunk_added(pool, b, n - GB)
                t, c = divmod(n, NCH)
                for s in range(SC):
                    pool.indirect_dma_start(
                        gat[:, n % GB, s, :], None, table,
                        bass.IndirectOffsetOnAxis(ap=idx[:, t, SC * c + s:SC * c + s + 1], axis=0),
                    ).then_inc(SEM[f"c_gather{n % GB}"], 16)

            def second(b, what, *a):
                if what == "pos":
                    wait(pool, "c_pos", b, 13)
                    wait(pool, "c_table", b, 64)
                    for n in range(GB - 1):
                        gather(b, n)
                elif what == "w":
                    t, = a
                    if t >= 2:
                        wait(pool, "c_prod", b, products(NCH * (t - 1) - 1))
                    for c in range(2):
                        ins = nc.gpsimd.tensor_tensor(
                            wlh[:, t % 2, :, c, :], ap3(wk[:, t, 2 * H:], [[1, S], [S, H]]),
                            ap3(frac[:, S * t:, c], [[2, S], [0, H]]), ALU.mult)
                    ins.then_inc(SEM["c_w"], 1)
                elif what == "g":
                    n = a[0] + GB - 1
                    if n < CHUNKS:
                        gather(b, n)

            run(pool, first, second)

        @block.scalar
        def _(act):
            act.wait_ge(setup["ready"], 1)
            act.wait_ge(loaded, 16 * n_loads)
            for h in range(H):
                nc.scalar.activation(emask[:, h % 4, h // 4, :], tri, ACT.Exp, scale=slope[:, h:h + 1])
            nc.scalar.activation(es[:], slope_c[:], ACT.Exp)
            act.wait_ge(setup["dve"], 8)
            for g in range(G):
                nc.scalar.activation(csT[:, g, :], ang[:, g, :], ACT.Sin).then_inc(setup["act"], 1)

            def log_exp():
                nc.scalar.preload_act_table_set("natural_log_exp_and_others")

            def copy_out(key, dst, b, view=None):
                src = wait_filled(act, key, b)
                nc.scalar.copy(dst, src[:, :] if view is None else view(src)).then_inc(empty(key), 1)

            def tiles(n):
                return lambda s: s[:, :].rearrange("p (a b) -> p a b", a=n)

            def first(b, what, *a):
                if what == "xT":
                    for j in range(J):
                        copy_out(("xT", j), xb[:, 1 + BLK * j:1 + BLK * (j + 1)], b)
                elif what == "kq":
                    i, = a
                    src = wait_filled(act, ("kq", i), b)
                    wait(act, "a_rot", b, i - 3)
                    nc.scalar.activation(silu4[:, i % 4, :], src[:, :], ACT.Silu, bias=kqb[:, i // 4, i % 2:i % 2 + 1]).then_inc(empty(("kq", i)), 1)
                elif what == "kt":
                    log_exp()
                    wait(act, "a_rot", b, 8)
                    for p in range(T // 2):
                        copy_out(("kt", p), silu4[:, p, :], b)
                elif what == "y":
                    att = wait_filled(act, ("att",), b)
                    for t in range(T):
                        nc.scalar.activation(yT[:, P * t:P * (t + 1)], att[:, t // TB, P * (t % TB):P * (t % TB + 1)], ACT.Square,
                                             accum_out=ss1[:, 0, t:t + 1]).then_inc(SEM["a_square"], 1)
                    wait(act, "a_square", b, T)
                    nc.scalar.activation(ss1[:, 1, :], ss1[:, 0, :], ACT.Ln, bias=col(REPS), scale=1.0 / D).then_inc(SEM["a_rstd"], 1)
                    wait(act, "a_rstd", b, 1)
                    nc.scalar.activation(ss1[:, 2, :], ss1[:, 1, :], ACT.Exp, scale=-0.5).then_inc(SEM["a_rstd"], 1)
                    for j in range(J):
                        copy_out(("yT", j), yT[:, BLK * j:BLK * (j + 1)], b)
                elif what == "mean":
                    m, = a
                    wait_drained(act, ("mean", m), b)
                    nc.scalar.activation(lnq[:, m % 2, :], lnc[:, m % 2, :], ACT.Square).then_inc(SEM["ln_square"], 1)
                elif what == "var":
                    m, = a
                    src = wait_filled(act, ("var", m), b)
                    nc.scalar.activation(lnq[:, m % 2, :], src[:, :], ACT.Ln, bias=col(EPS)).then_inc(empty(("var", m)), 1)
                    wait_drained(act, ("var", m), b)
                    nc.scalar.activation(lnq[:, m % 2, :], lnq[:, m % 2, :], ACT.Exp, scale=-0.5).then_inc(SEM["ln_rstd"], 1)
                    if 2 <= m < 6:
                        wait(act, "ln_out", b, m + 1)
                        nc.scalar.activation(hn[:, :], lnc[:, m % 2, :], ACT.Identity, bias=col(LB + m // 2 - 1)).then_inc(SEM["f_hn"], 1)
                elif what == "proj":
                    l, n = a
                    i = T * l + n
                    wait(act, "b_ss", b, 2 * i)
                    for w, key in enumerate((("qp", l, n), ("kp", l, n))):
                        src = wait_filled(act, key, b)
                        nc.scalar.activation(sq[:, w, :], src[:, :], ACT.Square).then_inc(SEM["b_square"], 1)
                elif what == "rn":
                    l, n = a
                    i = T * l + n
                    wait(act, "b_ss", b, 2 * i + 2)
                    nc.scalar.activation(ssq[:, n % 2, 1, :], ssq[:, n % 2, 0, :], ACT.Ln, scale=65536.0).then_inc(SEM["b_rn"], 1)
                    wait(act, "b_rn", b, 2 * i + 1)
                    nc.scalar.activation(ssq[:, n % 2, 1, :], ssq[:, n % 2, 1, :], ACT.Exp, bias=col(LN256), scale=-0.5).then_inc(SEM["b_rn"], 1)
                elif what == "v":
                    l, n = a
                    copy_out(("vp", l, n), vring[:, n % 3, :, 0:DH], b, tiles(HB))
                elif what == "turn":
                    l, n = a
                    copy_out(("qT", l, n), qTs[:, n % 2], b, tiles(PAIRS))
                    copy_out(("kT", l, n), keyT[:, n % 3], b, tiles(PAIRS))
                elif what == "X":
                    l, n = a
                    sc = wait_filled(act, ("S", l, n), b)
                    wait(act, "b_max", b, UNITS * l + n + 1)
                    for i in range(4):
                        ins = nc.scalar.activation(prob[:, n % 2, i, WIN:WIN + KEYS], sc[:, i // 2, KEYS * (i % 2):KEYS * (i % 2 + 1)],
                                                   ACT.Exp, bias=nmax[:, n % 2, i:i + 1])
                    ins.then_inc(empty(("S", l, n)), 1)
                elif what == "P":
                    l, n = a
                    copy_out(("Pc", l, n), PTc[:, n % 2], b, tiles(4))
                    copy_out(("Pp", l, n), PTp[:, n % 2], b, lambda s: s[:, 0:4 * WIN].rearrange("p (a b) -> p a b", a=4))
                elif what == "oT":
                    l, n = a
                    if n % TB == 0 and n:
                        wait_filled(act, ("wo", l, n // TB - 1), b)
                    copy_out(("oT", l, n), oT[:, :, P * (n % TB):P * (n % TB + 1)], b, tiles(4))
                elif what == "ff":
                    l, j, f = a
                    w, key = FW[f], ("gate", l, j, f)
                    src = wait_filled(act, key, b)
                    if f == 2:
                        wait_drained(act, ("up", l, j, 0), b)
                    nc.scalar.activation(gel(l, j, f)[0:w], src[0:w, :], ACT.Gelu, bias=col(BG + FB * l + f, w)).then_inc(empty(key), 1)
                    if f == FB - 1:
                        log_exp()

            def second(b, what, *a):
                if what == "x2t":
                    j, = a
                    if j == 0:
                        wait(act, "c_saved", b, 0)
                    copy_out(("x2t", j), x2tok[:, TB * j:TB * (j + 1), :], b, tiles(TB))
                elif what == "pos":
                    wait_drained(act, ("wk", T - 1), b)
                    nc.scalar.activation(wk[:], wk[:], ACT.Silu).then_inc(SEM["c_silu"], 1)
                    wait(act, "c_silu", b, 1)
                    nc.scalar.activation(sgt[:, 0], wk[:, :, 0:H], ACT.Sigmoid).then_inc(SEM["c_act"], 1)
                    nc.scalar.activation(sgt[:, 1], wk[:, :, H:2 * H], ACT.Tanh).then_inc(SEM["c_act"], 1)
                elif what == "cT":
                    copy_out(("sum", a[0]), cT[:, :], b)
                elif what == "co":
                    j, = a
                    src = wait_filled(act, ("co", j), b)
                    nc.scalar.activation(zc[:], src[:, :].rearrange("p (a b) -> p a b", a=TB), ACT.Silu).then_inc(empty(("co", j)), 1)
                    log_exp()
                    token_rstd(SEM["c_rstd"], lambda: wait(act, "c_bn", b, T * (j + 1)), lambda: wait(act, "c_rstd", b, 2 * j + 1), TB * j)
                elif what == "x3T":
                    copy_out(("x3T", a[0]), x3T[:, BLK * a[0]:BLK * (a[0] + 1)], b)
                elif what == "lg":
                    j, = a
                    src = wait_filled(act, ("lg", j), b)
                    if j == 0:
                        wait(act, "d_saved", b, 0)
                    nc.scalar.activation(lgS[:, BLK * j:BLK * (j + 1)], src[0:E_, :], ACT.Identity, bias=gb[:]).then_inc(empty(("lg", j)), 1)
                elif what == "soft":
                    wait(act, "d_max", b, 1)
                    nc.scalar.activation(lgS, lgS, ACT.Exp, bias=lgs[:, 0:1], accum_out=lgs[:, 1:2]).then_inc(SEM["d_exp"], 1)
                elif what == "iT":
                    for j in range(J):
                        copy_out(("iT", j), lgS[:, BLK * j:BLK * (j + 1)], b, lambda s: s[0:E_, :])
                elif what == "h1":
                    q, = a
                    src = wait_filled(act, ("h1", q), b)
                    nc.scalar.activation(h1s[:, q % 2, :], src[:, :], ACT.Relu, bias=col(C1 + q // 2)).then_inc(empty(("h1", q)), 1)
                elif what == "h2":
                    q, = a
                    src = wait_filled(act, ("h2", q), b)
                    nc.scalar.activation(h2s[:, q % 2, :], src[:, :], ACT.Relu, bias=col(C2 + q // 2)).then_inc(empty(("h2", q)), 1)
                elif what == "y":
                    q, = a
                    wait_drained(act, ("y", q), b)
                    nc.scalar.activation(ys[:, q % 4, :], ys[:, q % 4, :], ACT.Relu).then_inc(SEM["d_relu"], 1)

            def token_rstd(sem, stats, logs, at):
                ts = slice(at, at + TB)
                stats()
                nc.scalar.activation(rst[:, 0, ts], mv[:, ts, 1], ACT.Ln, bias=col(EPS)).then_inc(sem, 1)
                logs()
                nc.scalar.activation(rst[:, 1, ts], rst[:, 0, ts], ACT.Exp, scale=-0.5).then_inc(sem, 1)

            run(act, first, second)
            for i in range(B * J):
                token_rstd(last["rstd"], lambda: act.wait_ge(last["bn"], 2 * TB * (i + 1)), lambda: act.wait_ge(last["rstd"], 2 * i + 1), TB * (i % 2))

        @block.vector
        def _(dve):
            V = nc.vector
            dve.wait_ge(setup["ready"], 1)
            dve.wait_ge(loaded, 16 * n_loads)
            for g in range(G):
                V.tensor_scalar(ang[:, g, :], posr, col(TH + g), None, ALU.mult)
            V.tensor_copy(identb[:], ident[:]).then_inc(setup["dve"], 1)
            dve.wait_ge(setup["dve"], 1)
            V.tensor_scalar(kk[:, :, :], ang[:, :, :], col(PH), 0.15915494309189535, ALU.add, ALU.mult).then_inc(setup["dve"], 1)
            dve.wait_ge(setup["dve"], 2)
            V.tensor_scalar(kk[:, :, :], kk[:, :, :], ROUND, ROUND, ALU.add, ALU.subtract).then_inc(setup["dve"], 1)
            for i, part_of in enumerate((TWO_PI_HI, TWO_PI_MID, TWO_PI_LO)):
                dve.wait_ge(setup["dve"], 3 + i)
                V.scalar_tensor_tensor(ang[:, :, :], kk[:, :, :], -part_of, ang[:, :, :], ALU.mult, ALU.add).then_inc(setup["dve"], 1)
            dve.wait_ge(setup["dve"], 6)
            V.tensor_scalar(ang[:, :, :], ang[:, :, :], col(PH), PI_IN, ALU.add, ALU.min).then_inc(setup["dve"], 1)
            dve.wait_ge(setup["dve"], 7)
            for l in range(LAYERS):
                V.tensor_tensor(rot[:, l].rearrange("p t a b c -> p t (a b c)"), rbase,
                                ap3(qkscale[:, l, :], [[0, T], [1, 256]]), ALU.mult)
            V.tensor_scalar(ang[:, :, :], ang[:, :, :], -PI_IN, None, ALU.max).then_inc(setup["dve"], 1)

            def shift(dst, src, j, sem):
                V.tensor_copy(dst[0:64], src[0:64, 1 + BLK * j:1 + BLK * (j + 1)]).then_inc(SEM[sem], 1)
                V.tensor_copy(dst[64:P], src[64:P, BLK * j:BLK * (j + 1)]).then_inc(SEM[sem], 1)

            def block_of(x, j):
                return x[:, 1 + BLK * j:1 + BLK * (j + 1)]

            def polish(r, x, t, sem, done):
                V.scalar_tensor_tensor(t, x, -0.5, r, ALU.mult, ALU.mult).then_inc(sem, 1)
                done(1)
                V.tensor_tensor(t, t, r, ALU.mult).then_inc(sem, 1)
                done(2)
                V.scalar_tensor_tensor(r, t, 1.5, r, ALU.add, ALU.mult).then_inc(sem, 1)
                done(3)

            def first(b, what, *a):
                if what == "kq":
                    i, = a
                    j, g = i % 4 // 2, i % 2
                    wait_drained(dve, ("kq", i), b)
                    V.tensor_tensor((keyA, qryA)[i // 4][:, g, BLK * j:BLK * (j + 1)], silu4[:, i % 4, :],
                                    csT[:, g, BLK * j:BLK * (j + 1)], ALU.mult).then_inc(SEM["a_rot"], 1)
                elif what == "vu":
                    for p in range(T // 2):
                        src = wait_filled(dve, ("vu", p), b)
                        V.tensor_tensor(vu[:, 2 * p:2 * p + 2, :], src[:, :].rearrange("p (a b) -> p a b", a=2),
                                        ap3(vub[:], [[0, 2], [1, 2 * D]]), ALU.add).then_inc(empty(("vu", p)), 1)
                elif what == "KV":
                    for j in range(J):
                        src = wait_filled(dve, ("KV", j), b)
                        V.tensor_tensor(KV[:, TB * j:TB * (j + 1), :].rearrange("p t (g c) -> p (t g) c", g=G),
                                        src[:, :].rearrange("p (a b) -> p a b", b=D // G),
                                        ap3(blockd[:], [[0, TB * G], [1, D // G]]), ALU.mult).then_inc(empty(("KV", j)), 1)
                    wait_drained(dve, ("KV", J - 1), b)
                    V.memset(pre[:, 0, :], 0.0).then_inc(SEM["a_scan"], 1)
                    V.memset(suf[:, T - 1, :], 0.0).then_inc(SEM["a_scan"], 1)
                    for t in range(1, T):
                        wait(dve, "a_scan", b, 2 * t)
                        u = T - 1 - t
                        V.tensor_tensor(pre[:, t, :], pre[:, t - 1, :], KV[:, t - 1, :], ALU.add).then_inc(SEM["a_scan"], 1)
                        V.tensor_tensor(suf[:, u, :], suf[:, u + 1, :], KV[:, u + 1, :], ALU.add).then_inc(SEM["a_scan"], 1)
                    wait(dve, "a_scan", b, 16)
                    for g in range(G):
                        c = slice(64 * g, 64 * g + 64)
                        V.scalar_tensor_tensor(st[:, :, c], pre[:, :, c], es[:, g:g + 1], suf[:, :, c], ALU.mult, ALU.add).then_inc(SEM["a_state"], 1)
                elif what == "E":
                    p, = a
                    if p == 1:
                        wait(dve, "a_state", b, G)
                    for r in range(4):
                        src = wait_filled(dve, ("E", p, r), b)
                        em = em0 if p % 2 else silu4
                        V.tensor_tensor(em[:, r, :].rearrange("p (t g c) -> p t g c", t=2, g=G),
                                        src[:, :].rearrange("p (t g c) -> p t g c", t=2, g=G),
                                        ap3(emask[:, r, :, :], [[0, 2], [P, G], [1, P]]), ALU.mult).then_inc(empty(("E", p, r)), 1)
                elif what == "y":
                    att = wait_filled(dve, ("att",), b)
                    wait(dve, "a_rstd", b, 2)
                    ms = newt[:, 8:8 + T]
                    V.tensor_scalar(ms, ss1[:, 0, :], 1.0 / D, RMS_EPS, ALU.mult, ALU.add).then_inc(SEM["a_newton"], 1)
                    wait(dve, "a_newton", b, 1)
                    polish(ss1[:, 2, :], ms, newt[:, 0:T], SEM["a_newton"], lambda k: wait(dve, "a_newton", b, 1 + k))
                    for t in range(T):
                        ins = V.scalar_tensor_tensor(y[:, t, :], att[:, t // TB, P * (t % TB):P * (t % TB + 1)], ss1[:, 2, t:t + 1],
                                                     vu[:, t, D:2 * D], ALU.mult, ALU.mult)
                    ins.then_inc(empty(("att",)), 1)
                elif what == "ao":
                    for j in range(J):
                        src = wait_filled(dve, ("ao", j), b)
                        V.scalar_tensor_tensor(block_of(x1, j), src[:, :], col(OB), block_of(xb, j), ALU.add, ALU.add).then_inc(empty(("ao", j)), 1)
                elif what == "mean":
                    m, = a
                    src = block_of(x1 if m < 2 else xb, m % 2)
                    if 2 <= m < 6:
                        l, j = divmod(m - 2, 2)
                        wait_drained(dve, ("wo", l, j), b)
                        if m > 2:
                            pl, pj = divmod(m - 3, 2)
                            wait_drained(dve, ("up", pl, pj, FB - 1), b)
                        shift(h2, xm, j, "f_shift")
                        wait(dve, "f_shift", b, 2 * (m - 2) + 2)
                        src = h2[:, :]
                    elif m >= 6:
                        wait(dve, "f_res", b, m - 5)
                    mean = wait_filled(dve, ("mean", m), b)
                    V.tensor_tensor(lnc[:, m % 2, :], src, mean[:, :], ALU.subtract).then_inc(empty(("mean", m)), 1)
                elif what == "var":
                    m, = a
                    wait(dve, "ln_rstd", b, m + 1)
                    if m < 2:
                        V.tensor_tensor(block_of(x1, m), lnc[:, m % 2, :], lnq[:, m % 2, :], ALU.mult).then_inc(SEM["ln_out"], 1)
                    elif m < 6:
                        V.scalar_tensor_tensor(lnc[:, m % 2, :], lnc[:, m % 2, :], col(LG + m // 2 - 1), lnq[:, m % 2, :], ALU.mult, ALU.mult).then_inc(SEM["ln_out"], 1)
                    else:
                        V.tensor_tensor(x2[:, BLK * (m - 6):BLK * (m - 5)], lnc[:, m % 2, :], lnq[:, m % 2, :], ALU.mult).then_inc(SEM["ln_out"], 1)
                elif what == "shift":
                    l, j = a
                    if l == 0:
                        wait(dve, "ln_out", b, j + 1)
                    else:
                        wait_drained(dve, ("down", 0, j), b)
                    shift(hT[:, BLK * j:BLK * (j + 1)], (x1, xb)[l], j, "b_shift")
                elif what == "proj":
                    l, t = a
                    i = T * l + t
                    wait(dve, "b_square", b, 2 * i + 2)
                    V.tensor_reduce(ssq[:, t % 2, 0, :], sq[:, :, :].rearrange("p w (h d) -> p (w h) d", h=HB), AXX, ALU.add).then_inc(SEM["b_ss"], 1)
                    wait(dve, "b_ss", b, 2 * i + 1)
                    V.tensor_scalar(ssq[:, t % 2, 0, :], ssq[:, t % 2, 0, :], 1e-24, None, ALU.max).then_inc(SEM["b_ss"], 1)
                elif what == "rn":
                    normalize(b, *a)
                elif what == "rot":
                    rotate(b, *a)
                elif what == "S":
                    l, n = a
                    sc = wait_filled(dve, ("S", l, n), b)
                    V.tensor_reduce(nmax[:, n % 2, :], sc[:, :, 0:2 * KEYS].rearrange("p e (r k) -> p e r k", r=2), AXX, ALU.max,
                                    negate=True).then_inc(SEM["b_max"], 1)
                elif what == "O":
                    l, n = a
                    t, g = divmod(n, 2)
                    src = wait_filled(dve, ("O", l, n), b)[:, 0:4 * (DH + 1)].rearrange("p (i c) -> p i c", i=4)
                    V.reciprocal(rsum[:, n % 2, :], src[:, :, DH]).then_inc(SEM["b_recip"], 1)
                    wait(dve, "b_recip", b, UNITS * l + n + 1)
                    V.tensor_tensor(ap3(oS[:, t % 2, 256 * g:], [[DH, 2], [2 * DH, 2], [1, DH]]),
                                    src[:, :, 0:DH].rearrange("p (e r) c -> p e r c", e=2),
                                    ap3(rsum[:, n % 2, :], [[2, 2], [1, 2], [0, DH]]), ALU.mult).then_inc(empty(("O", l, n)), 1)
                elif what == "wo":
                    l, j = a
                    src = wait_filled(dve, ("wo", l, j), b)
                    V.tensor_tensor(block_of(xm, j), src[:, :], block_of((x1, xb)[l], j), ALU.add).then_inc(empty(("wo", l, j)), 1)
                elif what == "ff":
                    l, j, f = a
                    w, key = FW[f], ("up", l, j, f)
                    src = wait_filled(dve, key, b)
                    wait_drained(dve, ("gate", l, j, f), b)
                    V.scalar_tensor_tensor(up[0:w, f, :], src[0:w, :], col(BA + FB * l + f, w), gel(l, j, f)[0:w],
                                           ALU.add, ALU.mult).then_inc(empty(key), 1)
                elif what == "down":
                    l, j = a
                    key = ("down", l, j)
                    src = wait_filled(dve, key, b)
                    dst = block_of(xb, j)
                    V.scalar_tensor_tensor(dst, src[:, :], col(B2 + l), block_of(xm, j), ALU.add, ALU.add).then_inc(empty(key), 1)
                    if l == LAYERS - 1:
                        wait_drained(dve, key, b)
                        V.tensor_tensor(dst, dst, block_of(x1, j), ALU.add).then_inc(SEM["f_res"], 1)

            def normalize(b, l, t):
                i = T * l + t
                wait(dve, "b_rn", b, 2 * i + 2)
                polish(ssq[:, t % 2, 1, :], ssq[:, t % 2, 0, :], newt[:, 0:16], SEM["b_newton"], lambda k: wait(dve, "b_newton", b, 3 * i + k))
                for w, key in enumerate((("qp", l, t), ("kp", l, t))):
                    src = wait_filled(dve, key, b)
                    V.tensor_tensor(qn[:, w], src[:, :].rearrange("p (h d) -> p h d", h=HB),
                                    ap3(ssq[:, t % 2, 1, HB * w:HB * (w + 1)], [[1, HB], [0, DH]]), ALU.mult).then_inc(empty(key), 1)

            def rotate(b, l, t):
                i = T * l + t
                wait_drained(dve, ("kp", l, t), b)
                for s in range(2):
                    at, o = 32 * s, 32 * (1 - s)
                    V.tensor_tensor(r2[:, :, :, at:at + 32], qn[:, :, :, o:o + 32],
                                    ap3(rot[:, l, t, 1, 0, at:], [[DH, 2], [0, HB], [1, 32]]), ALU.mult).then_inc(SEM["b_sin"], 1)
                wait(dve, "b_sin", b, 2 * i + 2)
                V.tensor_tensor(qn, qn, ap3(rot[:, l, t, 0, 0, :], [[DH, 2], [0, HB], [1, DH]]), ALU.mult).then_inc(SEM["b_cos"], 1)
                wait(dve, "b_cos", b, i + 1)
                if i:
                    wait_filled(dve, ("kT", *divmod(i - 1, T)), b)
                V.tensor_tensor(qk.rearrange("p w c -> p (w c)"), qn.rearrange("p w h d -> p (w h d)"),
                                r2.rearrange("p w h d -> p (w h d)"), ALU.add).then_inc(SEM["b_qk"], 1)

            def token_polish(at, sem, done):
                ts = slice(at, at + TB)
                V.tensor_scalar(rst[:, 0, ts], mv[:, ts, 1], LN_EPS, None, ALU.add).then_inc(sem, 1)
                done(1)
                polish(rst[:, 1, ts], rst[:, 0, ts], newt[:, 0:TB], sem, lambda k: done(1 + k))

            def second(b, what, *a):
                if what == "wk":
                    t, = a
                    src = wait_filled(dve, ("wk", t), b)
                    V.tensor_tensor(wk[:, t, :], src[:, 0:CW], cb[:], ALU.add).then_inc(empty(("wk", t)), 1)
                elif what == "pos":
                    positions(b)
                elif what == "g":
                    n, = a
                    t, c = divmod(n, NCH)
                    if c == 0:
                        wait(dve, "c_w", b, t + 1)
                    wait(dve, f"c_gather{n % GB}", b, 16 * SC * (n // GB + 1))
                    g4 = gat[:, n % GB].rearrange("p s (c h d) -> p (s c) h d", c=2, h=H)
                    wv = ap3(wlh[:, t % 2, SC * c, 0, :], [[H, 2 * SC], [1, H], [0, HD]])
                    V.tensor_tensor(g4, g4, wv, ALU.mult).then_inc(SEM["c_prod"], 1)
                    if on_vector(n):
                        wait(dve, "c_prod", b, products(n) - 1)
                        before = n - 2 * SHARE
                        if before >= 0:
                            chunk_added(dve, b, before)
                        V.tensor_reduce(psums[:, n // SHARE % 2, :], ap3(gat[:, n % GB, 0, 0:1], [[1, D], [D, 2 * SC]]), AXX, ALU.add).then_inc(SEM["c_prod"], 1)
                elif what == "co":
                    j, = a
                    wait_drained(dve, ("co", j), b)
                    V.tensor_tensor(zc[:], zc[:], x2tok[:, TB * j:TB * (j + 1), :], ALU.add).then_inc(SEM["c_z"], 1)
                    wait(dve, "c_z", b, j + 1)
                    for t in range(TB * j, TB * (j + 1)):
                        V.bn_stats(bn[:, t, :], zc[:, t % TB, :]).then_inc(SEM["c_bn"], 1)
                    wait(dve, "c_bn", b, T * j + TB)
                    apart(dve)
                    for t in range(TB * j, TB * (j + 1)):
                        V.bn_aggr(mv[:, t, :], bn[:, t, :]).then_inc(SEM["c_bn"], 1)
                    wait(dve, "c_rstd", b, 2 * j + 2)
                    token_polish(TB * j, SEM["c_newton"], lambda k: wait(dve, "c_newton", b, 4 * j + k))
                    if j == 0:
                        wait(dve, "c_table", b, 64)
                    for t in range(TB * j, TB * (j + 1)):
                        V.tensor_scalar(x3[:, t, :], zc[:, t % TB, :], mv[:, t, 0:1], rst[:, 1, t:t + 1], ALU.subtract, ALU.mult).then_inc(SEM["c_x3"], 1)
                elif what == "soft":
                    wait_drained(dve, ("lg", J - 1), b)
                    V.tensor_reduce(lgs[:, 0:1], lgS, AXX, ALU.max, negate=True).then_inc(SEM["d_max"], 1)
                    wait(dve, "d_exp", b, 1)
                    V.reciprocal(lgs[:, 2:3], lgs[:, 1:2]).then_inc(SEM["d_max"], 1)
                    wait(dve, "d_max", b, 2)
                    V.tensor_scalar(lgS, lgS, lgs[:, 2:3], None, ALU.mult).then_inc(SEM["d_max"], 1)
                    src = wait_filled(dve, ("pT",), b)
                    V.tensor_copy(prT[:], src[:, 0:T * E_].rearrange("p (t e) -> p t e", t=T)).then_inc(empty(("pT",)), 1)
                elif what == "rank":
                    ranks(b)
                elif what == "y":
                    q, = a
                    src = wait_filled(dve, ("y", q), b)
                    e = q // 2
                    V.tensor_tensor(ys[:, q % 4, :].rearrange("p (t c) -> p t c", t=TB), src[:, :].rearrange("p (t c) -> p t c", t=TB),
                                    ap3(mw[:, e % 2, 3, :], [[0, TB], [1, D]]), ALU.add).then_inc(empty(("y", q)), 1)
                elif what == "vs":
                    q, = a
                    src = wait_filled(dve, ("vs", q), b)
                    if q >= 1:
                        wait_drained(dve, ("vs", q - 1), b)
                    V.tensor_tensor(vacc[:, q // 2:q // 2 + 1], vacc[:, q // 2:q // 2 + 1], src[:, 0:1], ALU.add).then_inc(empty(("vs", q)), 1)

            def positions(b):
                wait(dve, "c_act", b, 2)

                def step(i, ins):
                    ins.then_inc(SEM["c_pos"], 1)
                    wait(dve, "c_pos", b, i)

                step(1, V.tensor_reduce(fp[:, 0, :], sgt[:, 0], AXX, ALU.add))
                step(2, V.tensor_reduce(fp[:, 1, :], sgt[:, 1], AXX, ALU.add))
                step(3, V.tensor_scalar(fp[:, 2, :], fp[:, 0, :], 15.0 / H, 1.0, ALU.mult, ALU.add))
                step(4, V.scalar_tensor_tensor(fp[:, 3, :], fp[:, 1, :], 16.0 / H, base[:], ALU.mult, ALU.add))
                step(5, V.tensor_tensor(pos, ap3(sidx[:], [[0, T], [1, S]]), ap3(fp[:, 2, :], [[1, T], [0, S]]), ALU.mult))
                step(6, V.tensor_tensor(pos, pos, ap3(fp[:, 3, :], [[1, T], [0, S]]), ALU.add))
                step(7, V.tensor_scalar(pos, pos, 0.0, N - 1.0, ALU.max, ALU.min))
                step(8, V.tensor_scalar(lo, pos, ROUND, ROUND, ALU.add, ALU.subtract))
                step(9, V.tensor_tensor(frac[:, :, 0].rearrange("p (t s) -> p t s", t=T), lo, pos, ALU.is_gt))
                step(10, V.tensor_tensor(lo, lo, frac[:, :, 0].rearrange("p (t s) -> p t s", t=T), ALU.subtract))
                step(11, V.tensor_tensor(frac[:, :, 1].rearrange("p (t s) -> p t s", t=T), pos, lo, ALU.subtract))
                step(12, V.tensor_scalar(frac[:, :, 0], frac[:, :, 1], -1.0, 1.0, ALU.mult, ALU.add))
                V.tensor_scalar(idx[:], lo, 1.0, None, ALU.add).then_inc(SEM["c_pos"], 1)

            def ranks(b):
                other = ap3(prT[:], [[E_, T], [0, E_], [1, E_]])
                own = ap3(prT[:], [[E_, T], [1, E_], [0, E_]])
                wait_drained(dve, ("pT",), b)

                def step(i, ins):
                    ins.then_inc(SEM["d_rank"], 1)
                    wait(dve, "d_rank", b, i)

                step(1, V.tensor_tensor(rk1, other, own, ALU.is_gt))
                step(2, V.tensor_tensor(rk2, other, own, ALU.is_equal))
                step(3, V.tensor_tensor(rk2, rk2, ap3(ties[:], [[0, T], [E_, E_], [1, E_]]), ALU.mult))
                step(4, V.tensor_tensor(rk1, rk1, rk2, ALU.add))
                step(5, V.tensor_reduce(cnt[:], rk1.rearrange("p t e f -> p (t e) f"), AXX, ALU.add))
                step(6, V.tensor_scalar(ind[:], cnt[:], 1.5, None, ALU.is_lt))
                V.tensor_tensor(wt[:], ind[:].rearrange("p (t e) -> p t e", t=T), prT[:], ALU.mult).then_inc(SEM["d_rank"], 1)

            run(dve, first, second)
            dve.wait_ge(last["filled"], 1)
            V.tensor_copy(v8[:], psum["c0"][0:E_, 0:D]).then_inc(last["vt"], 1)
            for i in range(B * J):
                o = TB * (i % 2)
                dve.wait_ge(last["filled"], i + 2)
                dve.wait_ge(last[f"x{i % 2}"], 16 * (i // 2 + 1))
                xs = x2tok[:, o:o + TB, :]
                if i:
                    dve.wait_ge(last["out"], TB * i)
                V.tensor_tensor(zc[:], psum[CB[i % 2]][:, :].rearrange("p (a b) -> p a b", a=TB), xs, ALU.add).then_inc(last["z"], 1)
                dve.wait_ge(last["z"], i + 1)
                for t in range(TB):
                    V.bn_stats(bn[:, o + t, :], zc[:, t, :]).then_inc(last["bn"], 1)
                dve.wait_ge(last["bn"], 2 * TB * i + TB)
                for t in range(TB):
                    V.bn_aggr(mv[:, o + t, :], bn[:, o + t, :]).then_inc(last["bn"], 1)
                dve.wait_ge(last["rstd"], 2 * i + 2)
                token_polish(o, last["newton"], lambda k: dve.wait_ge(last["newton"], 4 * i + k))
                if i >= 2:
                    dve.wait_ge(last[f"stored{i % 2}"], 16 * (i // 2))
                for t in range(TB):
                    V.tensor_scalar(fin[:, o + t, :], zc[:, t, :], mv[:, o + t, 0:1], rst[:, 1, o + t:o + t + 1], ALU.subtract, ALU.mult).then_inc(last["out"], 1)

        @block.tensor
        def _(pe):
            pe.wait_ge(setup["ready"], 1)
            pe.wait_ge(loaded, 16 * n_loads)
            pe.wait_ge(setup["pool"], 1)
            pe.wait_ge(setup["dve"], 1)
            PE = nc.tensor
            mm = PE.matmul

            def turn_tiles(out, src, n=TB):
                for i in range(n):
                    ins = PE.transpose(out[:, P * i:P * (i + 1)], src(i), ident[:])
                return ins

            def first(b, what, *a):
                if what == "xT":
                    wait(pe, "x_loaded", b, 16)
                    for j in range(J):
                        out = wait_free(pe, ("xT", j), b)
                        turn_tiles(out, lambda i: xtok[:, TB * j + i, :]).then_inc(full(("xT", j)), 1)
                elif what == "kq":
                    i, = a
                    w, j, g = i // 4, i % 4 // 2, i % 2
                    wait_drained(pe, ("xT", j), b)
                    if i < 2:
                        apart(pe)
                    out = wait_free(pe, ("kq", i), b)
                    mm(out[:, :], wkq[:, w, P * g:P * (g + 1)], block_of(xb, j), start=True, stop=True).then_inc(full(("kq", i)), 1)
                elif what == "vu":
                    for p in range(T // 2):
                        out = wait_free(pe, ("vu", p), b)
                        for i in range(2):
                            t = 2 * p + i
                            ins = mm(out[:, 2 * D * i:2 * D * (i + 1)], xb[:, 1 + P * t:1 + P * (t + 1)], wvu[:], start=True, stop=True)
                        ins.then_inc(full(("vu", p)), 1)
                elif what == "kt":
                    for p in range(T // 2):
                        wait(pe, "a_rot", b, 2 * (p // 2) + 2)
                        out = wait_free(pe, ("kt", p), b)
                        turn_tiles(out, lambda i: keyA[:, i % 2, P * (2 * p + i // 2):P * (2 * p + i // 2 + 1)]).then_inc(full(("kt", p)), 1)
                elif what == "KV":
                    for j in range(J):
                        wait_drained(pe, ("vu", 2 * j + 1), b)
                        wait_drained(pe, ("kt", 2 * j + 1), b)
                        apart(pe)
                        out = wait_free(pe, ("KV", j), b)
                        for t in range(TB * j, TB * (j + 1)):
                            for g in range(G):
                                c = P * (t % TB) + 64 * g
                                ins = mm(out[:, c:c + 64], ktok[:, t, P * g:P * (g + 1)], vu[:, t, 64 * g:64 * g + 64], start=True, stop=True)
                        ins.then_inc(full(("KV", j)), 1)
                elif what == "E":
                    p, = a
                    wait(pe, "a_rot", b, 4 + 2 * (p // 2) + 2)
                    for r in range(4):
                        out = wait_free(pe, ("E", p, r), b)
                        for i in range(2):
                            for g in range(G):
                                c, t = 2 * P * i + P * g, 2 * p + i
                                ins = mm(out[:, c:c + P], keyA[32 * r:32 * r + 32, g, P * t:P * (t + 1)],
                                         qryA[32 * r:32 * r + 32, g, P * t:P * (t + 1)], start=True, stop=True)
                        ins.then_inc(full(("E", p, r)), 1)
                elif what == "heads":
                    p, = a
                    wait(pe, "a_state", b, G)
                    att = wait_free(pe, ("att",), b)
                    em = em0 if p % 2 else silu4
                    wait_drained(pe, ("E", p, 3), b)
                    for i in range(2):
                        t = 2 * p + i
                        out = att[:, t // TB, P * (t % TB):P * (t % TB + 1)]
                        for g in range(G):
                            mm(out[:, 64 * g:64 * g + 64], qryA[:, g, P * t:P * (t + 1)], st[:, t, 64 * g:64 * g + 64],
                               start=(t % TB == 0 and g == 0), stop=False, skip_group_check=True)
                        for h in range(H):
                            c = 2 * P * i + P * (h // 4)
                            ins = mm(out[:, HD * h:HD * (h + 1)], em[:, h % 4, c:c + P], vu[:, t, HD * h:HD * (h + 1)],
                                     start=False, stop=(t % TB == TB - 1 and h == H - 1), skip_group_check=True)
                    if p == T // 2 - 1:
                        ins.then_inc(full(("att",)), 1)
                elif what == "y":
                    wait_drained(pe, ("att",), b)
                    for j in range(J):
                        out = wait_free(pe, ("yT", j), b)
                        turn_tiles(out, lambda i: y[:, TB * j + i, :]).then_inc(full(("yT", j)), 1)
                elif what == "ao":
                    for j in range(J):
                        wait_drained(pe, ("yT", j), b)
                        out = wait_free(pe, ("ao", j), b)
                        mm(out[:, :], ow1[:], yT[:, BLK * j:BLK * (j + 1)], start=True, stop=True).then_inc(full(("ao", j)), 1)
                elif what == "mean":
                    m, = a
                    src = block_of(x1 if m < 2 else xb, m % 2)
                    if m < 2:
                        wait_drained(pe, ("ao", m), b)
                        apart(pe)
                    elif m < 6:
                        wait(pe, "f_shift", b, 2 * (m - 2) + 2)
                        src = h2[:, :]
                    else:
                        wait(pe, "f_res", b, m - 5)
                    out = wait_free(pe, ("mean", m), b)
                    mm(out[:, :], meanw[:], src, start=True, stop=True).then_inc(full(("mean", m)), 1)
                elif what == "var":
                    m, = a
                    wait(pe, "ln_square", b, m + 1)
                    out = wait_free(pe, ("var", m), b)
                    mm(out[:, :], meanw[:], lnq[:, m % 2, :], start=True, stop=True).then_inc(full(("var", m)), 1)
                elif what in ("proj", "v"):
                    l, n = a
                    wait(pe, "b_shift", b, 4 * l + 2 * (n // TB) + 2)
                    for name, c in ((("qp", 0), ("kp", INNER)) if what == "proj" else (("vp", 2 * INNER),)):
                        key = (name, l, n)
                        out = wait_free(pe, key, b)
                        mm(out[:, :], hT[:, P * n:P * (n + 1)], wqkv[:, l, c:c + INNER], start=True, stop=True).then_inc(full(key), 1)
                elif what == "turn":
                    l, n = a
                    wait(pe, "b_qk", b, T * l + n + 1)
                    for w, name in enumerate(("qT", "kT")):
                        out = wait_free(pe, (name, l, n), b)
                        turn_tiles(out, lambda i: qk[:, w, P * i:P * (i + 1)], PAIRS).then_inc(full((name, l, n)), 1)
                elif what == "S":
                    scores(b, *a)
                elif what == "P":
                    l, n = a
                    wait_drained(pe, ("S", l, n), b)
                    out = wait_free(pe, ("Pc", l, n), b)
                    turn_tiles(out, lambda i: prob[:, n % 2, i, P:2 * P]).then_inc(full(("Pc", l, n)), 1)
                    out = wait_free(pe, ("Pp", l, n), b)
                    apart(pe)
                    for i in range(4):
                        ins = PE.transpose(out[:, WIN * i:WIN * (i + 1)], prob[0:WIN, n % 2, i, 0:P], ident[0:WIN, 0:WIN])
                    ins.then_inc(full(("Pp", l, n)), 1)
                elif what == "O":
                    l, n = a
                    t, g = divmod(n, 2)
                    wait_drained(pe, ("Pp", l, n), b)
                    apart(pe)
                    out = wait_free(pe, ("O", l, n), b)
                    for i in range(4):
                        h, c = 4 * g + 2 * (i % 2) + i // 2, slice((DH + 1) * i, (DH + 1) * (i + 1))
                        mm(out[:, c], PTc[:, n % 2, i, :], vring[:, t % 3, h, :], start=True, stop=False, skip_group_check=True)
                        ins = mm(out[0:WIN, c], PTp[:, n % 2, i, :], vring[:, (t - 1) % 3, h, :], start=False, stop=True, skip_group_check=True)
                    ins.then_inc(full(("O", l, n)), 1)
                elif what == "oT":
                    l, n = a
                    wait_drained(pe, ("O", l, 2 * n + 1), b)
                    apart(pe)
                    out = wait_free(pe, ("oT", l, n), b)
                    turn_tiles(out, lambda i: oS[:, n % 2, P * i:P * (i + 1)]).then_inc(full(("oT", l, n)), 1)
                elif what == "wo":
                    l, n = a
                    wait_drained(pe, ("oT", l, TB * n + TB - 1), b)
                    out = wait_free(pe, ("wo", l, n), b)
                    for i in range(4):
                        ins = mm(out[:, :], wo[:, l, i, :], oT[:, i, :], start=(i == 0), stop=(i == 3))
                    ins.then_inc(full(("wo", l, n)), 1)
                elif what == "ff":
                    l, j, f = a
                    w = FW[f]
                    if f == 0:
                        wait(pe, "f_hn", b, 2 * l + j + 1)
                    for name, c in (("gate", HID + P * f), ("up", P * f)):
                        key = (name, l, j, f)
                        out = wait_free(pe, key, b)
                        mm(out[0:w, :], w1[:, l, c:c + w], hn[:, :], start=True, stop=True).then_inc(full(key), 1)
                elif what == "down":
                    l, j = a
                    key = ("down", l, j)
                    wait_drained(pe, ("up", l, j, FB - 1), b)
                    apart(pe)
                    out = wait_free(pe, key, b)
                    for f in range(FB):
                        w = FW[f]
                        ins = mm(out[:, :], w2[0:w, l, f, :], up[0:w, f, :], start=(f == 0), stop=(f == FB - 1))
                    ins.then_inc(full(key), 1)

            def block_of(x, j):
                return x[:, 1 + BLK * j:1 + BLK * (j + 1)]

            def scores(b, l, n):
                t, g = divmod(n, 2)
                if g == 0:
                    wait_drained(pe, ("kT", l, t), b)
                out = wait_free(pe, ("S", l, n), b)
                for e in range(2):
                    mm(out[:, e, 0:2 * KEYS], identb[:], ap3(band[:, min(t, 1), :], [[0, 2], [1, KEYS]]),
                       start=True, stop=False, skip_group_check=True)
                for e in range(2):
                    rows = slice(64 * e, 64 * e + 64)
                    for r in range(2):
                        pr, c = 2 * g + r, KEYS * r
                        q = qTs[rows, t % 2, pr, :]
                        mm(out[:, e, c:c + WIN], q, keyT[rows, (t - 1) % 3, pr, WIN:P], start=False, stop=False, skip_group_check=True)
                        ins = mm(out[:, e, c + WIN:c + KEYS], q, keyT[rows, t % 3, pr, :], start=False, stop=(r == 1), skip_group_check=True)
                ins.then_inc(full(("S", l, n)), 1)

            def second(b, what, *a):
                if what == "x2t":
                    j, = a
                    wait(pe, "ln_out", b, 7 + j)
                    out = wait_free(pe, ("x2t", j), b)
                    turn_tiles(out, lambda i: x2[:, BLK * j + P * i:BLK * j + P * (i + 1)]).then_inc(full(("x2t", j)), 1)
                elif what == "wk":
                    t, = a
                    out = wait_free(pe, ("wk", t), b)
                    mm(out[:, 0:CW], x2[:, P * t:P * (t + 1)], wc[:], start=True, stop=True).then_inc(full(("wk", t)), 1)
                elif what == "acc":
                    n, = a
                    j, i = divmod(n, BCH)
                    if i == 0:
                        wait_free(pe, ("sum", j), b)
                    out = psum[where[("sum", j)][0]]
                    wait(pe, "c_prod", b, products(n))
                    c = P * (i // NCH)
                    parts = [gat[:, n % GB, s, D * h:D * (h + 1)] for s in range(SC) for h in range(2)]
                    if on_vector(n):
                        parts = [psums[:, n // SHARE % 2, :]]
                    for k, x in enumerate(parts):
                        ins = mm(out[:, c:c + P], x, ident[:], start=(i == 0 and k == 0),
                                 stop=(i == BCH - 1 and k == len(parts) - 1), skip_group_check=True)
                    ins.then_inc(SEM["c_acc"] if i < BCH - 1 else full(("sum", j)), 1)
                elif what == "co":
                    j, = a
                    wait_drained(pe, ("sum", j), b)
                    apart(pe)
                    out = wait_free(pe, ("co", j), b)
                    for i in range(TB):
                        ins = mm(out[:, P * i:P * (i + 1)], cT[:, P * i:P * (i + 1)], ow2[:], start=True, stop=True)
                    ins.then_inc(full(("co", j)), 1)
                elif what == "x3T":
                    j, = a
                    wait(pe, "c_x3", b, TB * (j + 1))
                    out = wait_free(pe, ("x3T", j), b)
                    turn_tiles(out, lambda i: x3[:, TB * j + i, :]).then_inc(full(("x3T", j)), 1)
                elif what == "lg":
                    j, = a
                    wait_drained(pe, ("x3T", j), b)
                    apart(pe)
                    out = wait_free(pe, ("lg", j), b)
                    mm(out[0:E_, :], gw[:], x3T[:, BLK * j:BLK * (j + 1)], start=True, stop=True).then_inc(full(("lg", j)), 1)
                elif what == "soft":
                    wait(pe, "d_max", b, 3)
                    out = wait_free(pe, ("pT",), b)
                    apart(pe)
                    for t in range(T):
                        ins = PE.transpose(out[:, E_ * t:E_ * (t + 1)], lgS[:, P * t:P * (t + 1)], ident[0:E_, 0:E_])
                    ins.then_inc(full(("pT",)), 1)
                elif what == "iT":
                    wait(pe, "d_rank", b, 7)
                    for j in range(J):
                        out = wait_free(pe, ("iT", j), b)
                        for i in range(TB):
                            t = TB * j + i
                            ins = PE.transpose(out[0:E_, P * i:P * (i + 1)], ind[:, E_ * t:E_ * (t + 1)], ident[:])
                        ins.then_inc(full(("iT", j)), 1)
                elif what in ("h1", "h2", "y", "vs"):
                    expert(b, what, *a)

            def expert(b, what, q):
                e, j = divmod(q, 2)
                if what == "h1":
                    if j == 0:
                        wait(pe, f"d_expert{e % 2}", b, 32 * (e // 2 + 1))
                elif what == "h2":
                    wait_drained(pe, ("h1", q), b)
                    apart(pe)
                elif what == "y":
                    wait_drained(pe, ("h2", q), b)
                    apart(pe)
                else:
                    wait(pe, "d_relu", b, q + 1)
                out = wait_free(pe, (what, q), b)
                if what == "h1":
                    ins = mm(out[:, :], mw[:, e % 2, 0, :], x3T[:, BLK * j:BLK * (j + 1)], start=True, stop=True)
                elif what == "h2":
                    ins = mm(out[:, :], mw[:, e % 2, 1, :], h1s[:, q % 2, :], start=True, stop=True)
                elif what == "y":
                    for i in range(TB):
                        ins = mm(out[:, P * i:P * (i + 1)], h2s[:, q % 2, P * i:P * (i + 1)], mw[:, e % 2, 2, :], start=True, stop=True)
                else:
                    for i in range(TB):
                        ins = mm(out[:, 0:1], ys[:, q % 4, P * i:P * (i + 1)], wt[:, TB * j + i, e:e + 1], start=(i == 0), stop=(i == TB - 1))
                ins.then_inc(full((what, q)), 1)

            run(pe, first, second)
            for c in CB:
                pe.wait_ge(drained[c], (B + 1) * turns[c])
            PE.transpose(psum["c0"][0:E_, 0:D], vacc[:], ident[:]).then_inc(last["filled"], 1)
            pe.wait_ge(last["vt"], 1)
            pe.wait_ge(last["ind"], 16)
            for i in range(B * J):
                if i >= 2:
                    pe.wait_ge(last["z"], i - 1)
                for t in range(TB):
                    c = BLK * i + P * t
                    ins = mm(psum[CB[i % 2]][:, P * t:P * (t + 1)], indT[:, c:c + P], v8[:], start=True, stop=True)
                ins.then_inc(last["filled"], 1)


def kernel(**inputs):
    import numpy as np
    import concourse.bacc as _bacc
    from concourse.bass_utils import run_bass_kernel_spmd as _run

    f = lambda n: np.ascontiguousarray(np.asarray(inputs[n]))
    c = np.ascontiguousarray

    rows = np.array([(4 * g + r) * HD + d for g in range(G) for r in range(4) for _ in range(2) for d in range(HD)])
    w, wb = f("L0_attn_qkvu_w"), f("L0_attn_qkvu_b")
    host = {"x": f("L0_attn_x")}
    host["wkq"] = c(np.stack([w[D + rows].T, w[rows].T], 1))
    host["wvu"] = c(w[2 * D:].T)
    host["kqb"] = c(np.stack([wb[D + rows].reshape(G, P).T, wb[rows].reshape(G, P).T], 1))
    host["vub"] = c(wb[2 * D:])
    host["ow1"] = c(f("L0_attn_out_w").T)
    host["wqkv"] = c(f("L0_ffn_wqkv").transpose(1, 0, 2))
    host["wo"] = c(f("L0_ffn_wo").reshape(LAYERS, 4, P, D).transpose(2, 0, 1, 3))
    host["w1"] = c(f("L0_ffn_w1").transpose(1, 0, 2))

    def pad(a, n, axis):
        width = [(0, 0)] * a.ndim
        width[axis] = (0, n - a.shape[axis])
        return np.pad(a, width)

    host["w2"] = c(pad(f("L0_ffn_w2"), FB * P, 1).reshape(LAYERS, FB, P, D).transpose(2, 0, 1, 3))
    kw, kb = f("L1_attn_kernel_w").reshape(H, KS, D)[:, :S], f("L1_attn_kernel_b").reshape(H, KS)[:, :S]
    host["wc"] = c(np.concatenate([f("L1_attn_wave_w"), kw.reshape(H * S, D)]).T)
    host["cb"] = c(np.concatenate([f("L1_attn_wave_b"), kb.reshape(-1)]))
    host["ow2"] = c(f("L1_attn_out_w").T)
    host["gw"] = f("L1_ffn_gate_w")
    host["gb"] = f("L1_ffn_gate_b").reshape(E_, 1)
    host["experts"] = c(np.stack([f(f"L1_ffn_w{i}") for i in (1, 2, 3)], 2))
    host["b3"] = f("L1_ffn_b3").reshape(-1)
    slope = f("L0_attn_slope_rate").reshape(H)
    host["slope"] = slope
    host["slope_c"] = c(slope[rows // HD].reshape(G, P).T)
    theta = f("L0_attn_theta").reshape(-1)[rows].reshape(G, P).T
    b1 = pad(f("L0_ffn_b1").reshape(LAYERS, 2, HID), FB * P, 2).reshape(LAYERS, 2, FB, P)
    phase = np.tile(np.repeat(np.array([np.pi / 2, 0.0], np.float32), HD), 4).reshape(P, 1)
    ones = np.ones((P, 1), np.float32)
    columns = [f("L0_attn_out_b").reshape(P, 1), f("L0_ffn_ln_g").T, f("L0_ffn_ln_b").T,
               b1[:, 1].reshape(-1, P).T, b1[:, 0].reshape(-1, P).T, f("L0_ffn_b2").T,
               f("L1_ffn_b1").T, f("L1_ffn_b2").T, theta, phase,
               ones * np.float32(LN_EPS), ones * np.float32(RMS_EPS), ones * np.float32(np.log(256.0))]
    columns = np.concatenate(columns, 1)
    host["cols"] = c(pad(columns, 64, 1))
    qs, ks = f("L0_ffn_q_scale"), f("L0_ffn_k_scale")
    turn = (np.arange(DH) + DH // 2) % DH
    host["qkscale"] = c(np.stack([np.stack([qs, ks], 1), np.stack([qs[:, turn], ks[:, turn]], 1)], 1).reshape(LAYERS * 256))

    f4 = np.float32
    half_idx = np.arange(0, DH, 2, dtype=f4)
    inv_freq = (f4(1.0) / np.power(f4(10000.0), half_idx / f4(DH))).astype(f4)
    tt = np.arange(N, dtype=f4)
    freqs = (tt[:, None] * inv_freq[None, :]).astype(f4)
    freqs = np.concatenate([freqs, freqs], -1).astype(np.float64)
    bs = ((half_idx + f4(0.4 * DH)) / f4(1.4 * DH)).astype(np.float64)
    power = (tt.astype(np.float64) - N // 2) / float(WIN // 2)
    sc = bs[None, :] ** power[:, None]
    sc = np.concatenate([sc, sc], -1)
    sign = np.where(np.arange(DH) < DH // 2, -1.0, 1.0)[None]
    cs, sn = np.cos(freqs), np.sin(freqs) * sign
    tab = np.stack([cs * sc * 8.0, cs / sc, sn * sc * 8.0, sn / sc], 1).astype(f4)
    host["rbase"] = c(tab.reshape(T, P, 256).transpose(1, 0, 2))
    i, k = np.arange(P)[:, None], np.arange(KEYS)[None] - WIN
    seen = (k <= i) & (i <= k + WIN)
    import ml_dtypes
    bf = ml_dtypes.bfloat16
    host["band"] = c(np.stack([np.where(seen & (k >= 0), 0.0, MASKED), np.where(seen, 0.0, MASKED)], 1).astype(bf))
    host["ident"] = np.eye(P, dtype=f4)
    host["tri"] = (np.arange(P)[:, None] <= np.arange(P)[None]).astype(f4)
    host["blockd"] = (np.arange(P)[:, None] // 32 == np.arange(64)[None] // HD).astype(f4)
    host["posr"] = np.arange(N, dtype=f4)
    host["sidx"] = np.arange(S, dtype=f4) - 16
    host["base"] = c((np.arange(T)[None] * P + np.arange(P)[:, None]).astype(f4))
    host["ties"] = (np.arange(E_)[None] < np.arange(E_)[:, None]).astype(f4).reshape(-1)

    nc = _bacc.Bacc("TRN2", target_bir_lowering=False, num_devices=1)
    arrays, dram = {}, {}
    for name, a in host.items():
        arrays[f"in_{name}"] = a
        dram[name] = nc.dram_tensor(f"in_{name}", a.shape, mybir.dt.from_np(a.dtype), kind="ExternalInput").ap()
    out = nc.dram_tensor("out", (B, N, D), F32, kind="ExternalOutput").ap()

    def everywhere(row, n):
        return bass.AP(tensor=row.tensor, offset=row.offset, ap=[[0, P], [1, n]])

    def loads(v):
        full = lambda n: (v[n][:], dram[n])
        out_ = [full(n) for n in ("ident", "cols", "kqb", "wkq", "wvu", "slope_c", "blockd", "ow1", "wqkv", "wo", "w1", "w2", "wc", "ow2",
                                  "gw", "gb", "band", "base")]
        out_ += [(v["rbase"], dram["rbase"]), (v["tri"], dram["tri"])]
        for n in ("vub", "cb", "slope", "sidx"):
            out_.append((v[n][:], everywhere(dram[n], dram[n].shape[0])))
        out_.append((v["posr"], everywhere(dram["posr"], N)))
        out_.append((v["qkscale"].rearrange("p l c -> p (l c)"), everywhere(dram["qkscale"], LAYERS * 256)))
        out_.append((v["ties"][:].rearrange("p a b -> p (a b)"), everywhere(dram["ties"], E_ * E_)))
        return out_

    def batch_of(t, b):
        rows_ = t[b * N:(b + 1) * N] if isinstance(b, int) else t[bass.ds(b * N, N)]
        return rows_.rearrange("(t p) d -> p t d", p=P)

    A = {"x": dram["x"].rearrange("b n d -> (b n) d"), "loads": loads, "batch": batch_of, "flat": lambda t: t,
         "experts": dram["experts"], "b3": dram["b3"],
         "everywhere": lambda row, at, n: bass.AP(tensor=row.tensor, offset=row.offset + at, ap=[[0, P], [1, n]]),
         "outv": lambda i: out[i // J, BLK * (i % J):BLK * (i % J + 1)].rearrange("(t p) d -> p t d", p=P)}
    build(nc, A)
    r = _run(nc, [arrays], core_ids=[0])
    return r.results[0]["out"]
```
